# Optimizing a Trainium2 kernel written in Bass

```python
import numpy as np
import jax
import jax.numpy as jnp

def _softmax(x, axis=-1):
    return jax.nn.softmax(x, axis=axis)

def _gelu(x):
    return jax.nn.gelu(x, approximate=True)

def _silu(x):
    return jax.nn.silu(x)

def _sigmoid(x):
    return jax.nn.sigmoid(x)

def _layernorm(x, axis=-1, eps=1e-05):
    m = jnp.mean(x, axis=axis, keepdims=True)
    v = jnp.var(x, axis=axis, keepdims=True)
    return (x - m) / jnp.sqrt(v + eps)

def _scatter_add(tgt, idx, src, axis=0):
    return tgt.at[idx].add(src)

def _segment_sum(src, seg, n):
    return jax.ops.segment_sum(src, seg, n)
kernel_name = 'mk_decoder_postln_d1_seqx_r4_e05b19'

def setup_inputs(seed: int=0):
    np.random.seed(seed)
    _w = jnp.asarray

    def _rec_inputs():
        import jax
        import jax.numpy as jnp
        _rk = jax.random.key(seed)
        x = -0.0003929 + 0.9999 * jax.random.normal(jax.random.fold_in(_rk, 1), (16, 256, 256), jnp.float32)
        _lenS = 256 - jax.random.randint(jax.random.fold_in(_rk, 7), (16,), 0, max(1, 256 // 4) + 1, jnp.int32)
        _lenS2 = 256 - jax.random.randint(jax.random.fold_in(_rk, 8), (16,), 0, max(1, 256 // 4) + 1, jnp.int32)
        _ctx_1024P = jax.random.normal(jax.random.fold_in(_rk, 11), (16, 16, 256), jnp.float32)
        _ctx_1024c = jax.random.dirichlet(jax.random.fold_in(_rk, 511), 0.3 * jnp.ones((16,), jnp.float32), (16, 256))
        _ctx_1024t = jnp.einsum('bsk,bkd->bsd', _ctx_1024c, _ctx_1024P)
        _ctx_1024t = _ctx_1024t * jax.lax.rsqrt(jnp.mean(jnp.square(_ctx_1024t)) + 1e-12) * 0.953939
        ctx_1024 = -1.39393e-06 + 0.999914 * (_ctx_1024t + 0.3 * jax.random.normal(jax.random.fold_in(_rk, 611), (16, 256, 256), jnp.float32))
        return (x, ctx_1024)
    x, ctx_1024 = _rec_inputs()

    def _L0_attn_setup():
        import jax, jax.numpy as jnp
        import numpy as np
        import math
        D = 256
        H = 16
        HEAD_D = D // H
        T = 512
        B = 4
        key = jax.random.key(seed)
        k1, k2, k3 = jax.random.split(key, 3)
        x = jax.random.normal(k1, (B, T, D), dtype=jnp.float32)
        w_attn = jax.random.normal(k2, (D, D + 2 * HEAD_D), dtype=jnp.float32) * (1.0 / math.sqrt(D))
        w_proj = jax.random.normal(k3, (D, D), dtype=jnp.float32) * (1.0 / math.sqrt(D))
        return {'x': x, 'w_attn': w_attn, 'w_proj': w_proj}
    _L0_attn_all = _L0_attn_setup()
    _L0_attn_in = {k: v for k, v in _L0_attn_all.items() if k in ('w_attn', 'w_proj')}
    del _L0_attn_all

    def _L0_xattn_setup():
        import jax, jax.numpy as jnp
        import numpy as np
        HEADS = 16
        EPS = 1e-06

        def _rmsnorm(x, gamma):
            inv = jax.lax.rsqrt(jnp.mean(x * x, axis=-1, keepdims=True) + EPS)
            return x * inv * gamma
        key = jax.random.key(seed)
        ks = jax.random.split(key, 7)
        B, L, Lc, D, CTX = (4, 1024, 256, 256, 256)
        hd = D // HEADS
        s = 1.0 / np.sqrt(D)
        return {'x': jax.random.normal(ks[0], (B, L, D), jnp.float32), 'ctx': jax.random.normal(ks[1], (B, Lc, CTX), jnp.float32), 'Wq': jax.random.normal(ks[2], (D, D), jnp.float32) * s, 'Wkv': jax.random.normal(ks[3], (CTX, 2 * D), jnp.float32) * s, 'Wproj': jax.random.normal(ks[4], (D, D), jnp.float32) * s, 'q_gamma': jnp.ones((hd,), jnp.float32), 'k_gamma': jnp.ones((hd,), jnp.float32)}
    _L0_xattn_all = _L0_xattn_setup()
    _L0_xattn_in = {k: v for k, v in _L0_xattn_all.items() if k in ('Wq', 'Wkv', 'Wproj', 'q_gamma', 'k_gamma')}
    del _L0_xattn_all

    def _L0_ffn_setup():
        import jax, jax.numpy as jnp
        import numpy as np
        MAX_VAL = 100.0
        key = jax.random.key(seed)
        k1, k2, k3 = jax.random.split(key, 3)
        B, S, D_IN, D_OUT = (4, 2048, 256, 256)
        x = jax.random.normal(k1, (B, S, D_IN), dtype=jnp.float32)
        weights = jax.random.normal(k2, (D_OUT, D_IN), dtype=jnp.float32)
        scale = jnp.ones((D_OUT,), dtype=jnp.float32)
        bias = jax.random.normal(k3, (D_OUT,), dtype=jnp.float32)
        return {'x': x, 'weights': weights, 'scale': scale, 'bias': bias}
    _L0_ffn_all = _L0_ffn_setup()
    _L0_ffn_in = {k: v for k, v in _L0_ffn_all.items() if k in ('weights', 'scale', 'bias')}
    del _L0_ffn_all
    return {'x': x, 'ctx_1024': ctx_1024, 'L0_attn_w_attn': _L0_attn_in['w_attn'], 'L0_attn_w_proj': _L0_attn_in['w_proj'], 'L0_xattn_Wq': _L0_xattn_in['Wq'], 'L0_xattn_Wkv': _L0_xattn_in['Wkv'], 'L0_xattn_Wproj': _L0_xattn_in['Wproj'], 'L0_xattn_q_gamma': _L0_xattn_in['q_gamma'], 'L0_xattn_k_gamma': _L0_xattn_in['k_gamma'], 'L0_ffn_weights': _L0_ffn_in['weights'], 'L0_ffn_scale': _L0_ffn_in['scale'], 'L0_ffn_bias': _L0_ffn_in['bias']}

def reference(x, ctx_1024, L0_attn_w_attn, L0_attn_w_proj, L0_xattn_Wq, L0_xattn_Wkv, L0_xattn_Wproj, L0_xattn_q_gamma, L0_xattn_k_gamma, L0_ffn_weights, L0_ffn_scale, L0_ffn_bias):
    import jax
    import jax.numpy as jnp

    def _L0_attn_ref(x, w_attn, w_proj):
        import jax, jax.numpy as jnp
        import numpy as np
        import math
        D = 256
        H = 16
        HEAD_D = D // H
        T = 512
        B = 4
        Bv, Tv, _ = x.shape
        qkv = x @ w_attn
        q = qkv[..., :D].reshape(Bv, Tv, H, HEAD_D).transpose(0, 2, 1, 3)
        k = qkv[..., D:D + HEAD_D]
        v = qkv[..., D + HEAD_D:]
        scale = 1.0 / math.sqrt(HEAD_D)
        att = jnp.einsum('bhqd,bkd->bhqk', q, k) * scale
        causal = jnp.tril(jnp.ones((Tv, Tv), dtype=bool))
        att = jnp.where(causal[None, None, :, :], att, -jnp.inf)
        att = jax.nn.softmax(att, axis=-1)
        y = jnp.einsum('bhqk,bkd->bhqd', att, v)
        y = y.transpose(0, 2, 1, 3).reshape(Bv, Tv, D)
        return y @ w_proj

    def _L0_xattn_ref(x, ctx, Wq, Wkv, Wproj, q_gamma, k_gamma):
        import jax, jax.numpy as jnp
        import numpy as np
        HEADS = 16
        EPS = 1e-06

        def _rmsnorm(x, gamma):
            inv = jax.lax.rsqrt(jnp.mean(x * x, axis=-1, keepdims=True) + EPS)
            return x * inv * gamma
        B, L, D = x.shape
        Lc = ctx.shape[1]
        H = HEADS
        hd = D // H
        q = (x @ Wq).reshape(B, L, H, hd).transpose(0, 2, 1, 3)
        kv = (ctx @ Wkv).reshape(B, Lc, 2, H, hd).transpose(2, 0, 3, 1, 4)
        k, v = (kv[0], kv[1])
        q = _rmsnorm(q, q_gamma)
        k = _rmsnorm(k, k_gamma)
        scale = 1.0 / np.sqrt(hd)
        attn = jnp.einsum('bhld,bhmd->bhlm', q, k) * scale
        attn = jax.nn.softmax(attn, axis=-1)
        out = jnp.einsum('bhlm,bhmd->bhld', attn, v)
        out = out.transpose(0, 2, 1, 3).reshape(B, L, D)
        return out @ Wproj

    def _L0_ffn_ref(x, weights, scale, bias):
        import jax, jax.numpy as jnp
        import numpy as np
        MAX_VAL = 100.0
        w = (weights >= 0.0).astype(x.dtype) * 2.0 - 1.0
        y = jnp.einsum('bsi,oi->bso', x, w)
        y = y * scale + bias
        y = jnp.clip(y, -MAX_VAL, MAX_VAL)
        return y
    x = _layernorm(x + _L0_attn_ref(x, L0_attn_w_attn, L0_attn_w_proj), axis=-1)
    x = _layernorm(x + _L0_xattn_ref(x, ctx_1024, L0_xattn_Wq, L0_xattn_Wkv, L0_xattn_Wproj, L0_xattn_q_gamma, L0_xattn_k_gamma), axis=-1)
    x = _layernorm(x + _L0_ffn_ref(x, L0_ffn_weights, L0_ffn_scale, L0_ffn_bias), axis=-1)
    return x

_drawn_inputs = setup_inputs


def setup_inputs(seed=0):
    import zlib

    import numpy as np

    out = dict(_drawn_inputs(seed))
    spreads = {'L0_xattn_q_gamma': (1.0, 0.2),
     'L0_xattn_k_gamma': (1.0, 0.56),
     'L0_ffn_scale': (1.0, 0.2)}
    factors = {}
    for name, (base, spread) in spreads.items():
        noise = np.random.default_rng([zlib.crc32(name.encode()), seed]).standard_normal(out[name].shape)
        drawn = base * np.exp(spread * noise) if base else spread * noise
        out[name] = jnp.asarray(drawn.astype(out[name].dtype))
    for name, factor in factors.items():
        out[name] = (out[name] * factor).astype(out[name].dtype)
    return out
```

```python
import concourse.bass as bass
import concourse.mybir as mybir
from contextlib import ExitStack

F32 = mybir.dt.float32
BF16 = mybir.dt.bfloat16
ALU = mybir.AluOpType
ACT = mybir.ActivationFunctionType
AX = mybir.AxisListType

P = 128
B, T, D = 16, 256, 256
H = 16
HD = D // H
TT = T // P
DC = D // P
HC = H // DC
PARTS = 3
Q_SLOTS = (0, 1, 0, 1, 0, 2)
K_SLOTS = (0, 0, 1, 1, 2, 0)
QK_ROWS = len(Q_SLOTS) * HD
ROWS = QK_ROWS + 2
SCALE = HD ** -0.5
LN_EPS = 1e-5
RMS_EPS = 1e-6
CLIP = 100.0
MASKED = -1e30
NBANK = 3

BANKED = {"wT", "xT", "qS", "kS", "vS", "maxS", "mS", "t1S", "t2S", "t3S", "cT", "kv", "kX", "x1T", "q", "qX",
          "maxX", "mX", "t1X", "t2X", "t3X", "x2T", "ffn"}


def spread(main, extra, after):
    out, n, gaps = list(main[:after]), 0, len(main) - after
    for j, step in enumerate(main[after:]):
        out.append(step)
        upto = (j + 1) * len(extra) // gaps
        out += extra[n:upto]
        n = upto
    return out


def attention(tag, chunks, lag):
    out, half = [], chunks // 2
    for n in range(chunks + 2):
        if n < chunks:
            out.append(("qk" + tag, n, lag))
        if n >= 2:
            out.append(("pv" + tag, n - 2, lag))
            if (n - 2) % half == half - 1:
                out.append(("ot" + tag, (n - 2) // half, lag))
    return out


SELF_CHUNKS, CROSS_CHUNKS = 6, 8
MAX_S, MAX_X = 12, 16


def schedule():
    part_a = spread(attention("S", SELF_CHUNKS, 0),
                    [("x2T", 0, 2)] + [("maxX", u, 1) for u in range(8)] + [("ffn", 0, 2)]
                    + [("maxX", u, 1) for u in range(8, MAX_X)] + [("ln3", 0, 2), ("mX", 0, 1)], 2)
    part_b = [("t1S", 0, 0), ("t1S", 1, 0), ("xT", 0, -1), ("t2S", 0, 0), ("qS", 0, -1), ("kS", 0, -1),
              ("t3S", 0, 0), ("vS", 0, -1), ("cT", 0, 0), ("ln1", 0, 0), ("kv", 0, 0), ("qS2", 0, -1), ("kv", 1, 0),
              ("kn", 0, 0)]
    part_c = spread(attention("X", CROSS_CHUNKS, 1),
                    [("x1T", 0, 0), ("q", 0, 0), ("qn", 0, 0)] + [("maxS", u, -1) for u in range(MAX_S)]
                    + [("mS", 0, -1)], 4)
    part_d = [("t1X", 0, 1), ("t1X", 1, 1), ("kX", 0, 0), ("t2X", 0, 1), ("qX", 0, 0), ("t3X", 0, 1),
              ("kX2", 0, 0), ("qX2", 0, 0), ("ln2", 0, 1), ("keep", 0, 0)]
    loads = [("load_res", 0, 0), ("load_x", 0, -1), ("load_ctx", 0, 0)]
    return loads + part_a + part_b + part_c + part_d


SCHEDULE = schedule()
LOOP_FROM, LOOP_TO = 3, B - 1


def active(i, lag):
    return 0 <= i - lag < B


def bank_uses():
    uses, n = {}, 0
    uses[(-1, "wT", 0)] = n
    n += 1
    for i in range(-1, B + 2):
        for step, k, lag in SCHEDULE:
            if step in BANKED and active(i, lag):
                uses[(i, step, k)] = n
                n += 1
    return uses


BANK_USES = bank_uses()
USES = sum(step in BANKED for step, _, _ in SCHEDULE)
assert USES % NBANK == 0


def plus(i, per, c):
    if isinstance(i, int):
        return i * per + c
    e = i if per == 1 else i * per
    return e + c if c > 0 else e - (-c) if c < 0 else e


def bank_at(i, step, k, back=0):
    if isinstance(i, int):
        n = BANK_USES.get((i - back, step, k))
        return (0, None) if n is None else (n % NBANK, n // NBANK)
    n = BANK_USES[(LOOP_FROM, step, k)]
    return n % NBANK, plus(i, USES // NBANK, n // NBANK - (LOOP_FROM + back) * (USES // NBANK))


SIGNALS = {
    "x_in": 16, "ctx_in": 16, "x_res": 16,
    "qS_high": 1, "qS_mid": 1, "qS_low": 1,
    "kS_high": 1, "kS_mid": 1, "kS_low": 1,
    "qS_spilled": 16, "kX_spilled": 16, "qX_spilled": 16,
    "qS_stacked": 96, "kS_stacked": 96, "qX_stacked": 96, "kX_stacked": 96,
    "maxS_high": 1, "maxX_high": 1, "maxS_stacked": 32, "maxX_stacked": 32,
    "scoresS": SELF_CHUNKS, "expS": SELF_CHUNKS, "maskedS": SELF_CHUNKS, "pvS": 2, "otS": 2,
    "scoresX": CROSS_CHUNKS, "expX": CROSS_CHUNKS, "pvX": 2, "otX": 2,
    "rdenS": 2, "rdenX": 2,
    "k_sq": 1, "k_ss": 1, "k_ms": 1, "k_rs": 1, "k_norm": 1, "v_placed": 2,
    "q_sq": 1, "q_ss": 1, "q_ms": 1, "q_rs": 1, "q_norm": 1,
    "kX_high": 1, "kX_rest": 1, "kX_mid": 1, "kX_low": 1, "qX_high": 1, "qX_rest": 1, "qX_mid": 1, "qX_low": 1,
    "ln1_stats": 2, "ln1_aggr": 2, "ln1_var": 1, "ln1_rstd": 1, "x1": 2,
    "ln2_stats": 2, "ln2_aggr": 2, "ln2_var": 1, "ln2_rstd": 1, "x2": 2,
    "ln3_stats": 2, "ln3_aggr": 2, "ln3_var": 1, "ln3_rstd": 1, "x3": 2,
    "x1_kept": 1, "f_bias": 1, "f_clip": 1, "f_sum": 1, "stored": 16,
}


def decoder_program(nc, x, ctx_in_d, w_attn, w_proj, wq, wkv, wproj, q_gamma, k_gamma, ffn_w, ffn_scale, ffn_bias,
                    out, spill):
    es = ExitStack()
    with es:
        def sb(name, shape, dt=F32):
            return es.enter_context(nc.sbuf_tensor(name, shape, dt))

        def pb(name, shape):
            return es.enter_context(nc.psum_tensor(name, shape, F32))

        def sem(name):
            return es.enter_context(nc.semaphore(name))

        ident = sb("ident", [P, P])
        identb = sb("identb", [P, P], BF16)
        causal = sb("causal", [P, 4, P], BF16)
        halfpow = sb("halfpow", [P, TT * H])
        wa = sb("wa", [P, DC, D + 2 * HD])
        wp = sb("wp", [P, DC, D])
        wqx = sb("wqx", [P, DC, D])
        wkvx = sb("wkvx", [P, DC, 2 * D])
        wpx = sb("wpx", [P, DC, D])
        wf_raw = sb("wf_raw", [P, DC, D])
        wf_ge = sb("wf_ge", [P, DC, D])
        wf_sign = sb("wf_sign", [P, DC, D])
        wfT = sb("wfT", [P, DC, D])
        qg = sb("qg", [P, 1])
        kg = sb("kg", [P, 1])
        fscale = sb("fscale", [P, D])
        fbias = sb("fbias", [P, D])
        x_in = sb("x_in", [P, TT, D])
        x_res = sb("x_res", [P, TT, D])
        ctx = sb("ctx", [P, TT, D])
        x1 = sb("x1", [P, TT, D])
        x1_res = sb("x1_res", [P, TT, D])
        x2 = sb("x2", [P, TT, D])
        x3 = sb("x3", [P, TT, D])
        sum1 = sb("sum1", [P, TT, D])
        sum2 = sb("sum2", [P, TT, D])
        f1 = sb("f1", [P, TT, D])
        f2 = sb("f2", [P, TT, D])
        f3 = sb("f3", [P, TT, D])
        sum3 = sb("sum3", [P, TT, D])
        stats = {n: sb(f"stats{n}", [P, TT, 6]) for n in (1, 2, 3)}
        mv = {n: sb(f"mv{n}", [P, TT, 2]) for n in (1, 2, 3)}
        ve = {n: sb(f"ve{n}", [P, TT]) for n in (1, 2, 3)}
        rstd = {n: sb(f"rstd{n}", [P, TT]) for n in (1, 2, 3)}
        xT = sb("xT", [P, DC, T])
        ctxT = sb("ctxT", [P, DC, T])
        x1T = sb("x1T", [P, DC, T])
        x2T = sb("x2T", [P, DC, T])
        restS = sb("restS", [P, DC, T])
        partS = sb("partS", [P, DC, PARTS, T], BF16)
        restK = sb("restK", [HD, T])
        partK = sb("partK", [HD, PARTS, T], BF16)
        kvraw = sb("kvraw", [P, TT, 2 * D])
        qraw = sb("qraw", [P, TT, D])
        squares = {"k": sb("k_squares", [P, TT, D]), "q": sb("q_squares", [P, TT, D])}
        ss = {n: sb(n + "_ssum", [P, TT * H]) for n in "kq"}
        ms = {n: sb(n + "_msq", [P, TT * H]) for n in "kq"}
        rs = {n: sb(n + "_rsq", [P, TT * H]) for n in "kq"}
        normed = {n: sb(n + "_normed", [P, TT, D]) for n in "kq"}
        full = {n: sb(n + "_full", [P, DC, T]) for n in "kq"}
        restX = {n: sb(n + "_rest", [P, DC, T]) for n in "kq"}
        partX = {n: sb(n + "_parts", [P, DC, PARTS, T], BF16) for n in "kq"}
        qaS = sb("qaS", [ROWS, H, T], BF16)
        kaS = sb("kaS", [ROWS, T], BF16)
        qaX = sb("qaX", [ROWS, H, T], BF16)
        kaX = sb("kaX", [ROWS, H, T], BF16)
        maxS = sb("maxS", [P, TT, H])
        maxX = sb("maxX", [P, TT, H])
        negS = sb("negS", [H, 2, T], BF16)
        negX = sb("negX", [H, 2, T], BF16)
        ptS0 = sb("ptS0", [P, H, T])
        ptS1 = sb("ptS1", [P, H, P])
        ptX = sb("ptX", [P, TT, H, T])
        vaS = sb("vaS", [P, TT, 2 * HD])
        vaX = sb("vaX", [P, TT, H, 2 * HD])
        ot = {n: sb("ot" + n, [P, 4, T]) for n in "SX"}
        rden = {n: sb("rden" + n, [P, TT, H]) for n in "SX"}
        on = {n: sb("on" + n, [P, TT, D]) for n in "SX"}
        onT = {n: sb("onT" + n, [P, DC, T]) for n in "SX"}

        score = [pb(f"score{j}", [P, 1024]) for j in range(2)]
        out_bank = pb("out_bank", [P, 512])
        work = [pb(f"work{j}", [P, 512]) for j in range(NBANK)]

        filled = [sem(f"work{j}_filled") for j in range(NBANK)]
        drained = [sem(f"work{j}_drained") for j in range(NBANK)]
        signal = {name: sem(name) for name in SIGNALS}
        weights_in = sem("weights_in")
        ones_set = sem("ones_set")
        const_set = sem("const_set")
        sign_set = sem("sign_set")
        passed_dve = sem("passed_dve")
        passed_sp = sem("passed_sp")
        passed_pool = sem("passed_pool")

        def some(i, lag):
            return not isinstance(i, int) or i >= lag

        def count(i, lag, name, k=None):
            per = SIGNALS[name]
            if isinstance(i, int) and i - lag >= B:
                return B * per
            return plus(i, per, (per if k is None else k) - lag * per)

        class Use:

            def __init__(self, bank, before):
                self.bank, self.n = work[bank], before
                self.filled, self.drained = filled[bank], drained[bank]
                self.used = not isinstance(before, int) or before > 0

            def __getitem__(self, at):
                return self.bank[at]

        def use(i, step, k, back=0):
            bank, before = bank_at(i, step, k, back)
            return None if before is None else Use(bank, before)

        def run(eng, steps):
            def iteration(i):
                for step, k, lag in SCHEDULE:
                    if step in steps and (not isinstance(i, int) or active(i, lag)):
                        steps[step](i, k, lag)
            for i in range(-1, LOOP_FROM):
                iteration(i)
            with eng.Fori(LOOP_FROM, LOOP_TO) as i:
                iteration(i)
            for i in range(LOOP_TO, B + 2):
                iteration(i)

        n_weights = 16 * (6 + 2 * HC + 2)
        block = es.enter_context(nc.Block())

        @block.sync
        def _(sp):
            def rows(i, lag):
                return bass.ds(plus(i, T, -lag * T), T) if not isinstance(i, int) else slice((i - lag) * T, (i - lag + 1) * T)

            def tokens(ap, i, lag):
                return ap[rows(i, lag), :].rearrange("(t p) d -> p t d", p=P)

            def load(i, lag, dst, src, name):
                sp.dma_start(dst[:, :, :], tokens(src, i, lag)).then_inc(signal[name], 16)

            sp.dma_start(x_in[:, :, :], tokens(x, 0, 0)).then_inc(signal["x_in"], 16)
            for dst, src in ((wa, w_attn), (wqx, wq), (wkvx, wkv), (wp, w_proj), (wpx, wproj), (wf_raw, ffn_w)):
                sp.dma_start(dst[:, :, :], src.rearrange("(c p) n -> p c n", p=P)).then_inc(weights_in, 16)
            for dst, src in ((qg, q_gamma), (kg, k_gamma)):
                for h in range(HC):
                    sp.dma_start(dst[h * HD:(h + 1) * HD, :], src.rearrange("(d a) -> d a", a=1)).then_inc(weights_in, 16)
            for dst, src in ((fscale, ffn_scale), (fbias, ffn_bias)):
                sp.dma_start(dst[:, :], src.partition_broadcast(P)).then_inc(weights_in, 16)

            def load_x(i, k, lag):
                if not (isinstance(i, int) and i - lag == 0):
                    last = use(i, "xT", 0, back=1)
                    if last:
                        sp.wait_ge(last.filled, last.n + 1)
                        sp.sem_inc(passed_sp, 1)
                    load(i, lag, x_in, x, "x_in")

            def load_ctx(i, k, lag):
                last = use(i, "cT", 0, back=1)
                if last:
                    sp.wait_ge(last.filled, last.n + 1)
                    sp.sem_inc(passed_sp, 1)
                load(i, lag, ctx, ctx_in_d, "ctx_in")

            def load_res(i, k, lag):
                source = use(i, "t3S", 0, back=1)
                if source:
                    sp.wait_ge(source.drained, source.n + 1)
                    sp.sem_inc(passed_sp, 1)
                load(i, lag, x_res, x, "x_res")

            def restack(i, lag, parts, tag, slots, dst):
                sp.wait_ge(signal[tag + "_low"], count(i, lag, tag + "_low"))
                sp.sem_inc(passed_sp, 1)
                if some(i, lag + 1):
                    sp.wait_ge(signal[tag + "_stacked"], count(i, lag + 1, tag + "_stacked"))
                    sp.sem_inc(passed_sp, 1)
                sp.dma_start(spill[tag].rearrange("(c p) m -> p c m", p=P),
                             parts[:, :, :, :].rearrange("p c a t -> p c (a t)")).then_inc(signal[tag + "_spilled"], 16)
                sp.wait_ge(signal[tag + "_spilled"], count(i, lag, tag + "_spilled"))
                sp.sem_inc(passed_sp, 1)
                src = spill[tag].rearrange("(h d) (a t) -> d h a t", d=HD, a=PARTS)
                for s, part in enumerate(slots):
                    sp.dma_start(dst[s * HD:(s + 1) * HD, :, :], src[:, :, part, :]).then_inc(signal[tag + "_stacked"], 16)

            def qS2(i, k, lag):
                sp.wait_ge(signal["kS_low"], count(i, lag, "kS_low"))
                sp.sem_inc(passed_sp, 1)
                if some(i, lag + 1):
                    sp.wait_ge(signal["scoresS"], count(i, lag + 1, "scoresS"))
                    sp.sem_inc(passed_sp, 1)
                for s, part in enumerate(K_SLOTS):
                    sp.dma_start(kaS[s * HD:(s + 1) * HD, :], partK[:, part, :]).then_inc(signal["kS_stacked"], 16)
                restack(i, lag, partS, "qS", Q_SLOTS, qaS)

            def kX2(i, k, lag):
                if some(i, lag + 1):
                    sp.wait_ge(signal["scoresX"], count(i, lag + 1, "scoresX"))
                    sp.sem_inc(passed_sp, 1)
                restack(i, lag, partX["k"], "kX", K_SLOTS, kaX)

            def qX2(i, k, lag):
                restack(i, lag, partX["q"], "qX", Q_SLOTS, qaX)

            def max_rows(i, lag, tag, neg, dst):
                source = use(i, "m" + tag, 0)
                sp.wait_ge(source.drained, source.n + 1)
                sp.sem_inc(passed_sp, 1)
                for part in range(2):
                    sp.dma_start(dst[QK_ROWS + part:QK_ROWS + part + 1, :, :], neg[:, part, :])\
                        .then_inc(signal[f"max{tag}_stacked"], 16)

            def mS(i, k, lag):
                if some(i, lag + 1):
                    sp.wait_ge(signal["scoresS"], count(i, lag + 1, "scoresS"))
                    sp.sem_inc(passed_sp, 1)
                max_rows(i, lag, "S", negS, qaS)

            def mX(i, k, lag):
                if some(i, lag + 1):
                    sp.wait_ge(signal["scoresX"], count(i, lag + 1, "scoresX"))
                    sp.sem_inc(passed_sp, 1)
                max_rows(i, lag, "X", negX, qaX)

            def ln3(i, k, lag):
                sp.wait_ge(signal["x3"], count(i, lag, "x3"))
                sp.sem_inc(passed_sp, 1)
                sp.dma_start(tokens(out, i, lag), x3[:, :, :]).then_inc(signal["stored"], 16)

            run(sp, {"load_x": load_x, "load_ctx": load_ctx, "load_res": load_res, "qS2": qS2, "kX2": kX2, "qX2": qX2,
                     "mS": mS, "mX": mX, "ln3": ln3})
            sp.wait_ge(signal["stored"], 16 * B)

        @block.tensor
        def _(pe):
            def transpose_tokens(i, step, src):
                w = use(i, step, 0)
                if w.used:
                    pe.wait_ge(w.drained, w.n)
                for c in range(DC):
                    for t in range(TT):
                        mm = pe.transpose(w[:, c * T + t * P:c * T + (t + 1) * P], src[:, t, c * P:(c + 1) * P], ident[:, :])
                mm.then_inc(w.filled, 1)

            def project_tokens(i, step, k, srcT, weights, tile_at):
                w = use(i, step, k)
                if w.used:
                    pe.wait_ge(w.drained, w.n)
                n = weights.shape[2]
                for t, col in tile_at.items():
                    for c in range(DC):
                        mm = pe.matmul(w[:, col:col + n], srcT[:, c, t * P:(t + 1) * P], weights[:, c, :],
                                       start=(c == 0), stop=(c == DC - 1))
                mm.then_inc(w.filled, 1)

            def xT_(i, k, lag):
                pe.wait_ge(signal["x_in"], count(i, lag, "x_in"))
                transpose_tokens(i, "xT", x_in)

            def qS(i, k, lag):
                source = use(i, "xT", 0)
                pe.wait_ge(source.drained, source.n + 1)
                w = use(i, "qS", 0)
                if w.used:
                    pe.wait_ge(w.drained, w.n)
                for m in range(DC):
                    for c in range(DC):
                        mm = pe.matmul(w[:, m * T:(m + 1) * T], wa[:, c, m * P:(m + 1) * P], xT[:, c, :],
                                       start=(c == 0), stop=(c == DC - 1))
                mm.then_inc(w.filled, 1)

            def kS(i, k, lag):
                w = use(i, "kS", 0)
                if w.used:
                    pe.wait_ge(w.drained, w.n)
                for c in range(DC):
                    mm = pe.matmul(w[0:HD, 0:T], wa[:, c, D:D + HD], xT[:, c, :], start=(c == 0), stop=(c == DC - 1))
                mm.then_inc(w.filled, 1)

            def vS(i, k, lag):
                project_tokens(i, "vS", 0, xT, wa[:, :, D + HD:D + 2 * HD], {0: 0, 1: HD})

            def maxS_(i, u, lag):
                if u == 0:
                    pe.wait_ge(signal["qS_stacked"], count(i, lag, "qS_stacked"))
                    pe.wait_ge(signal["kS_stacked"], count(i, lag, "kS_stacked"))
                w = use(i, "maxS", u)
                if w.used:
                    pe.wait_ge(w.drained, w.n)
                if u < 8:
                    for j in range(2):
                        pe.matmul(w[:, j * T:(j + 1) * T], qaS[0:QK_ROWS, 2 * u + j, P:T], kaS[0:QK_ROWS, :],
                                  start=(j == 0), stop=False, skip_group_check=True)
                    mm = pe.matmul(w[:, :].rearrange("p (h k) -> p h k", h=2)[:, :, P:T], identb[:, :],
                                   causal[:, 0:2, :], start=False, stop=True, skip_group_check=True)
                else:
                    for j in range(4):
                        pe.matmul(w[:, j * P:(j + 1) * P], qaS[0:QK_ROWS, 4 * (u - 8) + j, 0:P], kaS[0:QK_ROWS, 0:P],
                                  start=(j == 0), stop=False, skip_group_check=True)
                    mm = pe.matmul(w[:, :], identb[:, :], causal[:, :, :].rearrange("p h k -> p (h k)"),
                                   start=False, stop=True, skip_group_check=True)
                mm.then_inc(w.filled, 1)

            def maxX_(i, u, lag):
                if u == 0:
                    pe.wait_ge(signal["qX_stacked"], count(i, lag, "qX_stacked"))
                    pe.wait_ge(signal["kX_stacked"], count(i, lag, "kX_stacked"))
                w = use(i, "maxX", u)
                if w.used:
                    pe.wait_ge(w.drained, w.n)
                t, h = u // 8, 2 * (u % 8)
                for j in range(2):
                    mm = pe.matmul(w[:, j * T:(j + 1) * T], qaX[0:QK_ROWS, h + j, t * P:(t + 1) * P],
                                   kaX[0:QK_ROWS, h + j, :], start=True, stop=True)
                mm.then_inc(w.filled, 1)

            def turn_max(i, step, last, src):
                source = use(i, *last)
                pe.wait_ge(source.drained, source.n + 1)
                w = use(i, step, 0)
                if w.used:
                    pe.wait_ge(w.drained, w.n)
                for t in range(TT):
                    mm = pe.matmul(w[0:H, t * P:(t + 1) * P], src[:, t, :], ident[:, :], start=True, stop=True)
                mm.then_inc(w.filled, 1)

            def score_slot(i, lag, tag, other, other_lag, n):
                if n >= 2:
                    pe.wait_ge(signal["exp" + tag], count(i, lag, "exp" + tag, n - 1))
                else:
                    if some(i, other_lag):
                        pe.wait_ge(signal["exp" + other], count(i, other_lag, "exp" + other))
                return score[n % 2]

            def qkS(i, n, lag):
                if n == 0:
                    pe.wait_ge(signal["maxS_stacked"], count(i, lag, "maxS_stacked"))
                s = score_slot(i, lag, "S", "X", lag + 2, n)
                if n % 3 < 2:
                    g = 2 * (n // 3) + n % 3
                    for j in range(2):
                        mm = pe.matmul(s[:, j * 512:(j + 1) * 512], kaS[:, 0:P],
                                       qaS[:, 4 * g + 2 * j:4 * g + 2 * j + 2, :], start=True, stop=True)
                else:
                    h = 8 * (n // 3)
                    for j in range(2):
                        mm = pe.matmul(s[:, j * 512:(j + 1) * 512], kaS[:, P:T],
                                       qaS[:, h + 4 * j:h + 4 * j + 4, P:T], start=True, stop=True)
                mm.then_inc(signal["scoresS"], 1)

            def qkX(i, n, lag):
                if n == 0:
                    pe.wait_ge(signal["maxX_stacked"], count(i, lag, "maxX_stacked"))
                s = score_slot(i, lag, "X", "S", lag - 1, n)
                g, kt = n // 2, n % 2
                for j in range(4):
                    h = 4 * g + j
                    mm = pe.matmul(s[:, j * T:(j + 1) * T], kaX[:, h, kt * P:(kt + 1) * P], qaX[:, h, :],
                                   start=True, stop=True)
                mm.then_inc(signal["scoresX"], 1)

            def pvS(i, n, lag):
                half = n // 3
                pe.wait_ge(signal["maskedS"], count(i, lag, "maskedS", n + 1))
                if n == 0:
                    source = use(i, "vS", 0, back=1)
                    if source:
                        pe.wait_ge(source.drained, source.n + 1)
                    if some(i, lag + 2):
                        pe.wait_ge(signal["otX"], count(i, lag + 2, "otX"))
                if n == 3:
                    pe.wait_ge(signal["otS"], count(i, lag, "otS", 1))
                if n % 3 < 2:
                    g = 2 * half + n % 3
                    for j in range(4):
                        pe.matmul(out_bank[32 * j:32 * (j + 1), (n % 3) * T:(n % 3 + 1) * T], vaS[:, 0, :],
                                  ptS0[:, 4 * g + j, :], start=(n % 3 == 0), stop=False, skip_group_check=True)
                else:
                    for gg in range(2):
                        for j in range(4):
                            mm = pe.matmul(out_bank[32 * j:32 * (j + 1), gg * T + P:(gg + 1) * T], vaS[:, 1, :],
                                           ptS1[:, 8 * half + 4 * gg + j, :], start=False, stop=True,
                                           skip_group_check=True)
                    mm.then_inc(signal["pvS"], 1)

            def pvX(i, n, lag):
                g, kt = n // 2, n % 2
                pe.wait_ge(signal["expX"], count(i, lag, "expX", n + 1))
                if n == 0:
                    pe.wait_ge(signal["v_placed"], count(i, lag, "v_placed"))
                    if some(i, lag - 1):
                        pe.wait_ge(signal["otS"], count(i, lag - 1, "otS"))
                if n == 4:
                    pe.wait_ge(signal["otX"], count(i, lag, "otX", 1))
                for j in range(4):
                    h = 4 * g + j
                    mm = pe.matmul(out_bank[32 * j:32 * (j + 1), (g % 2) * T:(g % 2 + 1) * T], vaX[:, kt, h, :],
                                   ptX[:, kt, h, :], start=(kt == 0), stop=(kt == 1), skip_group_check=True)
                if n % 4 == 3:
                    mm.then_inc(signal["pvX"], 1)

            def t1(tag):
                def step(i, t, lag):
                    pe.wait_ge(signal["ot" + tag], count(i, lag, "ot" + tag))
                    w = use(i, "t1" + tag, t)
                    if w.used:
                        pe.wait_ge(w.drained, w.n)
                    for g in range(4):
                        mm = pe.transpose(w[:, g * P:(g + 1) * P], ot[tag][:, g, t * P:(t + 1) * P], ident[:, :])
                    mm.then_inc(w.filled, 1)
                return step

            def t2(tag):
                def step(i, k, lag):
                    source = use(i, "t1" + tag, 1)
                    pe.wait_ge(source.drained, source.n + 1)
                    transpose_tokens(i, "t2" + tag, on[tag])
                return step

            def t3(tag, weights):
                def step(i, k, lag):
                    source = use(i, "t2" + tag, 0)
                    pe.wait_ge(source.drained, source.n + 1)
                    project_tokens(i, "t3" + tag, 0, onT[tag], weights, {0: 0, 1: D})
                return step

            def cT(i, k, lag):
                pe.wait_ge(signal["ctx_in"], count(i, lag, "ctx_in"))
                transpose_tokens(i, "cT", ctx)

            def kv(i, t, lag):
                source = use(i, "cT", 0)
                pe.wait_ge(source.drained, source.n + 1)
                project_tokens(i, "kv", t, ctxT, wkvx, {t: 0})

            def kX(i, k, lag):
                pe.wait_ge(signal["k_norm"], count(i, lag, "k_norm"))
                transpose_tokens(i, "kX", normed["k"])

            def x1T_(i, k, lag):
                pe.wait_ge(signal["x1"], count(i, lag, "x1"))
                transpose_tokens(i, "x1T", x1)

            def q_(i, k, lag):
                source = use(i, "x1T", 0)
                pe.wait_ge(source.drained, source.n + 1)
                project_tokens(i, "q", 0, x1T, wqx, {0: 0, 1: D})

            def qX(i, k, lag):
                pe.wait_ge(signal["q_norm"], count(i, lag, "q_norm"))
                transpose_tokens(i, "qX", normed["q"])

            def x2T_(i, k, lag):
                pe.wait_ge(signal["x2"], count(i, lag, "x2"))
                transpose_tokens(i, "x2T", x2)

            def ffn(i, k, lag):
                source = use(i, "x2T", 0)
                pe.wait_ge(source.drained, source.n + 1)
                project_tokens(i, "ffn", 0, x2T, wfT, {0: 0, 1: D})

            pe.wait_ge(const_set, 5)
            pe.wait_ge(ones_set, 5)
            pe.wait_ge(weights_in, n_weights)
            pe.wait_ge(sign_set, 2)
            for c in range(DC):
                for o in range(DC):
                    mm = pe.transpose(work[0][:, c * D + o * P:c * D + (o + 1) * P], wf_sign[:, o, c * P:(c + 1) * P],
                                      ident[:, :])
            mm.then_inc(filled[0], 1)

            run(pe, {"xT": xT_, "qS": qS, "kS": kS, "vS": vS, "maxS": maxS_, "maxX": maxX_,
                     "mS": lambda i, k, lag: turn_max(i, "mS", ("maxS", MAX_S - 1), maxS),
                     "mX": lambda i, k, lag: turn_max(i, "mX", ("maxX", MAX_X - 1), maxX),
                     "qkS": qkS, "qkX": qkX, "pvS": pvS, "pvX": pvX, "t1S": t1("S"), "t1X": t1("X"),
                     "t2S": t2("S"), "t2X": t2("X"), "t3S": t3("S", wp), "t3X": t3("X", wpx), "cT": cT, "kv": kv,
                     "kX": kX, "x1T": x1T_, "q": q_, "qX": qX, "x2T": x2T_, "ffn": ffn})

        @block.scalar
        def _(act):
            def flat(tile):
                return tile[:, :, :].rearrange("p c t -> p (c t)")

            def copy_out(step, dst, product, product_k=0):
                def emit(i, k, lag):
                    last = use(i, product, product_k, back=1)
                    if last:
                        act.wait_ge(last.filled, last.n + 1)
                    w = use(i, step, 0)
                    act.wait_ge(w.filled, w.n + 1)
                    act.activation(flat(dst), w[:, :], ACT.Copy).then_inc(w.drained, 1)
                return emit

            def kv(i, t, lag):
                if some(i, lag + 1):
                    act.wait_ge(signal["k_norm"], count(i, lag + 1, "k_norm"))
                    act.wait_ge(signal["v_placed"], count(i, lag + 1, "v_placed"))
                w = use(i, "kv", t)
                act.wait_ge(w.filled, w.n + 1)
                act.activation(kvraw[:, t, :], w[:, :], ACT.Copy).then_inc(w.drained, 1)

            def q_(i, k, lag):
                if some(i, lag + 1):
                    act.wait_ge(signal["q_norm"], count(i, lag + 1, "q_norm"))
                w = use(i, "q", 0)
                act.wait_ge(w.filled, w.n + 1)
                act.activation(flat(qraw), w[:, :], ACT.Copy).then_inc(w.drained, 1)

            def qS(i, k, lag):
                w = use(i, "qS", 0)
                act.wait_ge(w.filled, w.n + 1)
                if some(i, lag + 1):
                    act.wait_ge(signal["qS_spilled"], count(i, lag + 1, "qS_spilled"))
                act.activation(partS[:, :, 0, :], w[:, :].rearrange("p (c t) -> p c t", c=DC), ACT.Copy)\
                    .then_inc(signal["qS_high"], 1)

            def kS(i, k, lag):
                w = use(i, "kS", 0)
                act.wait_ge(w.filled, w.n + 1)
                if some(i, lag + 1):
                    act.wait_ge(signal["kS_stacked"], count(i, lag + 1, "kS_stacked"))
                act.activation(partK[:, 0, :], w[0:HD, 0:T], ACT.Copy).then_inc(signal["kS_high"], 1)

            def vS(i, k, lag):
                if some(i, lag + 1):
                    act.wait_ge(signal["pvS"], count(i, lag + 1, "pvS"))
                w = use(i, "vS", 0)
                act.wait_ge(w.filled, w.n + 1)
                act.wait_ge(ones_set, 5)
                act.activation(vaS[:, :, 0:HD], w[:, 0:TT * HD].rearrange("p (t d) -> p t d", t=TT), ACT.Copy)\
                    .then_inc(w.drained, 1)
                source = use(i, "qS", 0)
                act.wait_ge(source.drained, source.n + 1)
                act.activation(partS[:, :, 1, :], restS[:, :, :], ACT.Copy).then_inc(signal["qS_mid"], 1)
                source = use(i, "kS", 0)
                act.wait_ge(source.drained, source.n + 1)
                act.activation(partK[:, 1, :], restK[:, :], ACT.Copy).then_inc(signal["kS_mid"], 1)

            def neg_high(tag, neg):
                def emit(i, k, lag):
                    w = use(i, "m" + tag, 0)
                    act.wait_ge(w.filled, w.n + 1)
                    if some(i, lag + 1):
                        act.wait_ge(signal[f"max{tag}_stacked"], count(i, lag + 1, f"max{tag}_stacked"))
                    act.activation(neg[:, 0, :], w[0:H, 0:T], ACT.Copy, scale=-1.0)\
                        .then_inc(signal[f"max{tag}_high"], 1)
                return emit

            def expS(i, n, lag):
                act.wait_ge(signal["scoresS"], count(i, lag, "scoresS", n + 1))
                if some(i, lag + 1):
                    act.wait_ge(signal["pvS"], count(i, lag + 1, "pvS", n // 3 + 1))
                if n % 3 < 2:
                    g = 2 * (n // 3) + n % 3
                    dst = ptS0[:, 4 * g:4 * g + 4, :]
                else:
                    dst = ptS1[:, 8 * (n // 3):8 * (n // 3) + 8, :]
                act.activation(dst.rearrange("p h q -> p (h q)"), score[n % 2][:, :], ACT.Exp, scale=SCALE)\
                    .then_inc(signal["expS"], 1)

            def expX(i, n, lag):
                act.wait_ge(signal["scoresX"], count(i, lag, "scoresX", n + 1))
                if some(i, lag + 1):
                    act.wait_ge(signal["pvX"], count(i, lag + 1, "pvX", n // 4 + 1))
                g, kt = n // 2, n % 2
                act.activation(ptX[:, kt, 4 * g:4 * g + 4, :].rearrange("p h q -> p (h q)"), score[n % 2][:, :],
                               ACT.Exp, scale=SCALE).then_inc(signal["expX"], 1)

            def otev(tag):
                def emit(i, half, lag):
                    act.wait_ge(signal["pv" + tag], count(i, lag, "pv" + tag, half + 1))
                    last = use(i, "t1" + tag, 1, back=1)
                    if last:
                        act.wait_ge(last.filled, last.n + 1)
                    act.activation(ot[tag][:, 2 * half:2 * half + 2, :].rearrange("p g t -> p (g t)"), out_bank[:, :],
                                   ACT.Copy).then_inc(signal["ot" + tag], 1)
                return emit

            def square(n, src, step, last_k):
                def emit(i, k, lag):
                    source = use(i, step, last_k)
                    act.wait_ge(source.drained, source.n + 1)
                    if some(i, lag + 1):
                        act.wait_ge(signal[n + "_ss"], count(i, lag + 1, n + "_ss"))
                    act.activation(squares[n][:, :, :], src, ACT.Square).then_inc(signal[n + "_sq"], 1)
                return emit

            def parts(n, gamma):
                def emit(i, k, lag):
                    w = use(i, n + "X", 0)
                    act.wait_ge(w.filled, w.n + 1)
                    if some(i, lag + 1):
                        act.wait_ge(signal[n + "X_low"], count(i, lag + 1, n + "X_low"))
                    act.activation(full[n][:, :, :].rearrange("p c t -> p (c t)"), w[:, :], ACT.Copy,
                                   scale=gamma[:, 0:1]).then_inc(w.drained, 1)
                    source = use(i, n + "X", 0)
                    act.wait_ge(source.drained, source.n + 1)
                    if some(i, lag + 1):
                        act.wait_ge(signal[n + "X_spilled"], count(i, lag + 1, n + "X_spilled"))
                    act.activation(partX[n][:, :, 0, :], full[n][:, :, :], ACT.Copy).then_inc(signal[n + "X_high"], 1)
                return emit

            def mid(n):
                def emit(i, k, lag):
                    act.wait_ge(signal[n + "X_rest"], count(i, lag, n + "X_rest"))
                    act.activation(partX[n][:, :, 1, :], restX[n][:, :, :], ACT.Copy).then_inc(signal[n + "X_mid"], 1)
                return emit

            act.wait_ge(weights_in, n_weights)
            act.wait_ge(filled[0], 1)
            act.activation(wfT[:, :, :].rearrange("p c o -> p (c o)"), work[0][:, :], ACT.Copy).then_inc(drained[0], 1)

            run(act, {
                "xT": copy_out("xT", xT, "vS"), "qS": qS, "kS": kS, "vS": vS,
                "cT": copy_out("cT", ctxT, "kv", 1), "kv": kv, "kn": square("k", kvraw[:, :, 0:D], "kv", 1),
                "kX": parts("k", kg), "kX2": mid("k"), "qX": parts("q", qg), "qX2": mid("q"),
                "x1T": copy_out("x1T", x1T, "q"), "q": q_, "qn": square("q", qraw[:, :, :], "q", 0),
                "x2T": copy_out("x2T", x2T, "ffn"),
                "t2S": copy_out("t2S", onT["S"], "t3S"), "t2X": copy_out("t2X", onT["X"], "t3X"),
                "mS": neg_high("S", negS), "mX": neg_high("X", negX),
                "qkS": expS, "qkX": expX, "otS": otev("S"), "otX": otev("X"),
            })

        @block.vector
        def _(dve):
            dve.memset(halfpow[:, :], -0.5).then_inc(ones_set, 1)
            dve.memset(kaS[QK_ROWS:ROWS, :], 1.0).then_inc(ones_set, 1)
            dve.memset(kaX[QK_ROWS:ROWS, :, :].rearrange("p h t -> p (h t)"), 1.0).then_inc(ones_set, 1)
            dve.memset(vaS[:, :, :], 1.0).then_inc(ones_set, 1)
            dve.memset(vaX[:, :, :, :].rearrange("p t h d -> p (t h d)"), 1.0).then_inc(ones_set, 1)
            dve.wait_ge(weights_in, n_weights)
            dve.tensor_scalar(wf_ge[:, :, :], wf_raw[:, :, :], 0.0, 2.0, ALU.is_ge, ALU.mult).then_inc(sign_set, 1)
            dve.wait_ge(sign_set, 1)
            dve.tensor_scalar(wf_sign[:, :, :], wf_ge[:, :, :], -1.0, None, ALU.add).then_inc(sign_set, 1)

            def qS(i, k, lag):
                w = use(i, "qS", 0)
                dve.wait_ge(w.filled, w.n + 1)
                dve.wait_ge(signal["qS_high"], count(i, lag, "qS_high"))
                if some(i, lag + 1):
                    dve.wait_ge(signal["qS_low"], count(i, lag + 1, "qS_low"))
                dve.tensor_tensor(restS[:, :, :], w[:, :].rearrange("p (c t) -> p c t", c=DC), partS[:, :, 0, :],
                                  ALU.subtract).then_inc(w.drained, 1)

            def kS(i, k, lag):
                w = use(i, "kS", 0)
                dve.wait_ge(w.filled, w.n + 1)
                dve.wait_ge(signal["kS_high"], count(i, lag, "kS_high"))
                if some(i, lag + 1):
                    dve.wait_ge(signal["kS_low"], count(i, lag + 1, "kS_low"))
                dve.tensor_tensor(restK[:, :], w[0:HD, 0:T], partK[:, 0, :], ALU.subtract).then_inc(w.drained, 1)

            def vS(i, k, lag):
                dve.wait_ge(signal["qS_mid"], count(i, lag, "qS_mid"))
                dve.tensor_tensor(partS[:, :, 2, :], restS[:, :, :], partS[:, :, 1, :], ALU.subtract)\
                    .then_inc(signal["qS_low"], 1)
                dve.wait_ge(signal["kS_mid"], count(i, lag, "kS_mid"))
                dve.tensor_tensor(partK[:, 2, :], restK[:, :], partK[:, 1, :], ALU.subtract)\
                    .then_inc(signal["kS_low"], 1)

            def maxS_(i, u, lag):
                if u == 0:
                    last = use(i, "mS", 0, back=1)
                    if last:
                        dve.wait_ge(last.filled, last.n + 1)
                w = use(i, "maxS", u)
                dve.wait_ge(w.filled, w.n + 1)
                if u < 8:
                    dve.tensor_reduce(maxS[:, 1, 2 * u:2 * u + 2], w[:, :].rearrange("p (h k) -> p h k", h=2), AX.X,
                                      ALU.max).then_inc(w.drained, 1)
                else:
                    dve.tensor_reduce(maxS[:, 0, 4 * (u - 8):4 * (u - 8) + 4], w[:, :].rearrange("p (h k) -> p h k", h=4),
                                      AX.X, ALU.max).then_inc(w.drained, 1)

            def maxX_(i, u, lag):
                if u == 0:
                    last = use(i, "mX", 0, back=1)
                    if last:
                        dve.wait_ge(last.filled, last.n + 1)
                w = use(i, "maxX", u)
                dve.wait_ge(w.filled, w.n + 1)
                t, h = u // 8, 2 * (u % 8)
                dve.tensor_reduce(maxX[:, t, h:h + 2], w[:, :].rearrange("p (h k) -> p h k", h=2), AX.X, ALU.max)\
                    .then_inc(w.drained, 1)

            def neg_low(tag, neg):
                def emit(i, k, lag):
                    w = use(i, "m" + tag, 0)
                    dve.wait_ge(w.filled, w.n + 1)
                    dve.wait_ge(signal[f"max{tag}_high"], count(i, lag, f"max{tag}_high"))
                    if some(i, lag + 1):
                        dve.wait_ge(signal[f"max{tag}_stacked"], count(i, lag + 1, f"max{tag}_stacked"))
                    dve.scalar_tensor_tensor(neg[:, 1, :], w[0:H, 0:T], -1.0, neg[:, 0, :], ALU.mult, ALU.subtract)\
                        .then_inc(w.drained, 1)
                return emit

            def normalise(tag):
                def emit(i, t, lag):
                    w = use(i, "t1" + tag, t)
                    dve.wait_ge(w.filled, w.n + 1)
                    last = use(i, "t2" + tag, 0, back=1)
                    if last:
                        dve.wait_ge(last.filled, last.n + 1)
                    o = w[:, :].rearrange("p (h e) -> p h e", e=2 * HD)
                    dve.reciprocal(rden[tag][:, t, :], o[:, :, HD]).then_inc(signal["rden" + tag], 1)
                    dve.wait_ge(signal["rden" + tag], count(i, lag, "rden" + tag, t + 1))
                    dve.tensor_tensor(on[tag][:, t, :].rearrange("p (h d) -> p h d", d=HD), o[:, :, 0:HD],
                                      rden[tag][:, t, :].unsqueeze(2).to_broadcast([P, H, HD]), ALU.mult)\
                        .then_inc(w.drained, 1)
                return emit

            def moments(i, lag, n, src):
                for t in range(TT):
                    dve.bn_stats(stats[n][:, t, :], src[:, t, :]).then_inc(signal[f"ln{n}_stats"], 1)
                for t in range(TT):
                    dve.wait_ge(signal[f"ln{n}_stats"], count(i, lag, f"ln{n}_stats", t + 1))
                    dve.sem_inc(passed_dve, 1)
                    dve.bn_aggr(mv[n][:, t, :], stats[n][:, t, :]).then_inc(signal[f"ln{n}_aggr"], 1)

            def residual(tag, n, total, res, res_ready):
                def emit(i, k, lag):
                    w = use(i, "t3" + tag, 0)
                    dve.wait_ge(w.filled, w.n + 1)
                    dve.wait_ge(signal[res_ready], count(i, lag, res_ready))
                    if some(i, lag + 1):
                        dve.wait_ge(signal[f"x{n}"], count(i, lag + 1, f"x{n}"))
                    dve.tensor_tensor(total[:, :, :].rearrange("p t d -> p (t d)"), w[:, :],
                                      res[:, :, :].rearrange("p t d -> p (t d)"), ALU.add).then_inc(w.drained, 1)
                    dve.wait_ge(w.drained, w.n + 1)
                    moments(i, lag, n, total)
                return emit

            def apply_norm(i, lag, n, src, dst):
                dve.wait_ge(signal[f"ln{n}_rstd"], count(i, lag, f"ln{n}_rstd"))
                for t in range(TT):
                    dve.tensor_scalar(dst[:, t, :], src[:, t, :], mv[n][:, t, 0:1], rstd[n][:, t:t + 1],
                                      ALU.subtract, ALU.mult).then_inc(signal[f"x{n}"], 1)

            def ln1(i, k, lag):
                if some(i, lag + 1):
                    dve.wait_ge(signal["x1_kept"], count(i, lag + 1, "x1_kept"))
                last = use(i, "x1T", 0, back=1)
                if last:
                    dve.wait_ge(last.filled, last.n + 1)
                apply_norm(i, lag, 1, sum1, x1)

            def ln2(i, k, lag):
                if some(i, lag + 1):
                    dve.wait_ge(signal["f_sum"], count(i, lag + 1, "f_sum"))
                apply_norm(i, lag, 2, sum2, x2)

            def ln3(i, k, lag):
                if some(i, lag + 1):
                    dve.wait_ge(signal["stored"], count(i, lag + 1, "stored"))
                apply_norm(i, lag, 3, sum3, x3)

            def sum_squares(n):
                def emit(i, k, lag):
                    dve.wait_ge(signal[n + "_sq"], count(i, lag, n + "_sq"))
                    if some(i, lag + 1):
                        dve.wait_ge(signal[n + "_ms"], count(i, lag + 1, n + "_ms"))
                    dve.tensor_reduce(ss[n][:, :], squares[n][:, :, :].rearrange("p t (h d) -> p (t h) d", d=HD), AX.X,
                                      ALU.add).then_inc(signal[n + "_ss"], 1)
                return emit

            def rms(n, src, step):
                def emit(i, k, lag):
                    dve.wait_ge(signal[n + "_rs"], count(i, lag, n + "_rs"))
                    last = use(i, step, 0, back=1)
                    if last:
                        dve.wait_ge(last.filled, last.n + 1)
                    dve.tensor_tensor(normed[n][:, :, :].rearrange("p t (h d) -> p t h d", d=HD),
                                      src.rearrange("p t (h d) -> p t h d", d=HD),
                                      rs[n][:, :].rearrange("p (t h) -> p t h", t=TT).unsqueeze(3)
                                      .to_broadcast([P, TT, H, HD]), ALU.mult).then_inc(signal[n + "_norm"], 1)
                return emit

            def rest(n):
                def emit(i, k, lag):
                    dve.wait_ge(signal[n + "X_high"], count(i, lag, n + "X_high"))
                    dve.tensor_tensor(restX[n][:, :, :], full[n][:, :, :], partX[n][:, :, 0, :], ALU.subtract)\
                        .then_inc(signal[n + "X_rest"], 1)
                return emit

            def low(n):
                def emit(i, k, lag):
                    dve.wait_ge(signal[n + "X_mid"], count(i, lag, n + "X_mid"))
                    dve.tensor_tensor(partX[n][:, :, 2, :], restX[n][:, :, :], partX[n][:, :, 1, :], ALU.subtract)\
                        .then_inc(signal[n + "X_low"], 1)
                return emit

            def ffn(i, k, lag):
                w = use(i, "ffn", 0)
                dve.wait_ge(w.filled, w.n + 1)
                if some(i, lag + 1):
                    dve.wait_ge(signal["f_bias"], count(i, lag + 1, "f_bias"))
                dve.tensor_tensor(f1[:, :, :], w[:, :].rearrange("p (t d) -> p t d", t=TT),
                                  fscale[:, :].unsqueeze(1).to_broadcast([P, TT, D]), ALU.mult).then_inc(w.drained, 1)
                source = use(i, "ffn", 0)
                dve.wait_ge(source.drained, source.n + 1)
                dve.tensor_tensor(f2[:, :, :], f1[:, :, :], fbias[:, :].unsqueeze(1).to_broadcast([P, TT, D]),
                                  ALU.add).then_inc(signal["f_bias"], 1)
                dve.wait_ge(signal["f_bias"], count(i, lag, "f_bias"))
                dve.tensor_scalar(f3[:, :, :], f2[:, :, :], -CLIP, CLIP, ALU.max, ALU.min).then_inc(signal["f_clip"], 1)
                dve.wait_ge(signal["f_clip"], count(i, lag, "f_clip"))
                dve.tensor_tensor(sum3[:, :, :], f3[:, :, :], x2[:, :, :], ALU.add).then_inc(signal["f_sum"], 1)
                dve.wait_ge(signal["f_sum"], count(i, lag, "f_sum"))
                moments(i, lag, 3, sum3)

            run(dve, {
                "qS": qS, "kS": kS, "vS": vS, "maxS": maxS_, "maxX": maxX_,
                "mS": neg_low("S", negS), "mX": neg_low("X", negX), "t1S": normalise("S"), "t1X": normalise("X"),
                "t3S": residual("S", 1, sum1, x_res, "x_res"), "t3X": residual("X", 2, sum2, x1_res, "x1_kept"),
                "ln1": ln1, "ln2": ln2, "ln3": ln3,
                "kn": sum_squares("k"), "qn": sum_squares("q"),
                "kX": lambda i, k, lag: (rms("k", kvraw[:, :, 0:D], "kX")(i, k, lag), rest("k")(i, k, lag)),
                "qX": lambda i, k, lag: (rms("q", qraw[:, :, :], "qX")(i, k, lag), rest("q")(i, k, lag)),
                "kX2": low("k"), "qX2": low("q"), "ffn": ffn,
            })

        @block.gpsimd
        def _(pool):
            def gate():
                pool.sem_inc(passed_pool, 1)

            pool.wait_ge(ones_set, 5)
            pool.memset(ident[:, :], 0.0).then_inc(const_set, 1)
            pool.wait_ge(const_set, 1)
            pool.affine_select(out=ident[:, :], in_=ident[:, :], compare_op=ALU.not_equal, fill=1.0, base=0,
                               pattern=[[-1, P]], channel_multiplier=1).then_inc(const_set, 1)
            pool.wait_ge(const_set, 2)
            pool.tensor_copy(identb[:, :], ident[:, :]).then_inc(const_set, 1)
            pool.memset(causal[:, :, :], 0.0).then_inc(const_set, 1)
            pool.wait_ge(const_set, 4)
            pool.affine_select(out=causal[:, :, :], in_=causal[:, :, :], compare_op=ALU.is_ge, fill=MASKED, base=0,
                               pattern=[[0, 4], [-1, P]], channel_multiplier=1).then_inc(const_set, 1)

            def mask(i, n, lag):
                pool.wait_ge(signal["expS"], count(i, lag, "expS", n + 1))
                gate()
                if n % 3 < 2:
                    g = 2 * (n // 3) + n % 3
                    pt, heads = ptS0[:, 4 * g:4 * g + 4, 0:P], 4
                else:
                    pt, heads = ptS1[:, 8 * (n // 3):8 * (n // 3) + 8, :], 8
                pool.affine_select(out=pt, in_=pt, compare_op=ALU.is_ge, fill=0.0, base=0,
                                   pattern=[[0, heads], [1, P]], channel_multiplier=-1).then_inc(signal["maskedS"], 1)

            def inverse_root(i, lag, n):
                pool.wait_ge(signal[n + "_ss"], count(i, lag, n + "_ss"))
                if some(i, lag + 1):
                    pool.wait_ge(signal[n + "_rs"], count(i, lag + 1, n + "_rs"))
                gate()
                pool.tensor_scalar(ms[n][:, :], ss[n][:, :], 1.0 / HD, RMS_EPS, ALU.mult, ALU.add)\
                    .then_inc(signal[n + "_ms"], 1)
                if some(i, lag + 1):
                    pool.wait_ge(signal[n + "_norm"], count(i, lag + 1, n + "_norm"))
                pool.wait_ge(signal[n + "_ms"], count(i, lag, n + "_ms"))
                pool.tensor_tensor(rs[n][:, :], ms[n][:, :], halfpow[:, :], ALU.pow).then_inc(signal[n + "_rs"], 1)

            def kn(i, k, lag):
                inverse_root(i, lag, "k")

            def place_v(i, k, lag):
                if some(i, lag + 1):
                    pool.wait_ge(signal["pvX"], count(i, lag + 1, "pvX"))
                source = use(i, "kv", 1)
                pool.wait_ge(source.drained, source.n + 1)
                for t in range(TT):
                    gate()
                    pool.tensor_copy(vaX[:, t, :, 0:HD], kvraw[:, t, D:2 * D].rearrange("p (h d) -> p h d", d=HD))\
                        .then_inc(signal["v_placed"], 1)

            def rstd_of(n):
                def emit(i, lag):
                    pool.wait_ge(signal[f"ln{n}_aggr"], count(i, lag, f"ln{n}_aggr"))
                    if some(i, lag + 1):
                        pool.wait_ge(signal[f"ln{n}_rstd"], count(i, lag + 1, f"ln{n}_rstd"))
                    gate()
                    pool.tensor_scalar(ve[n][:, :], mv[n][:, :, 1], LN_EPS, None, ALU.add)\
                        .then_inc(signal[f"ln{n}_var"], 1)
                    if some(i, lag + 1):
                        pool.wait_ge(signal["x%d" % n], count(i, lag + 1, "x%d" % n))
                    pool.wait_ge(signal[f"ln{n}_var"], count(i, lag, f"ln{n}_var"))
                    pool.tensor_tensor(rstd[n][:, :], ve[n][:, :], halfpow[:, 0:TT], ALU.pow)\
                        .then_inc(signal[f"ln{n}_rstd"], 1)
                return emit

            def keep_x1(i, lag):
                pool.wait_ge(signal["x1"], count(i, lag, "x1"))
                source = use(i, "t3X", 0)
                if source:
                    pool.wait_ge(source.drained, source.n + 1)
                gate()
                pool.tensor_copy(x1_res[:, :, :], x1[:, :, :]).then_inc(signal["x1_kept"], 1)

            run(pool, {
                "qkS": mask, "t3S": lambda i, k, lag: rstd_of(1)(i, lag), "kn": kn,
                "qn": lambda i, k, lag: inverse_root(i, lag, "q"),
                "kX2": place_v,
                "t3X": lambda i, k, lag: rstd_of(2)(i, lag),
                "ffn": lambda i, k, lag: rstd_of(3)(i, lag),
                "keep": lambda i, k, lag: keep_x1(i, lag),
            })


_IN = ["x", "ctx_1024", "L0_attn_w_attn", "L0_attn_w_proj", "L0_xattn_Wq", "L0_xattn_Wkv", "L0_xattn_Wproj",
       "L0_xattn_q_gamma", "L0_xattn_k_gamma", "L0_ffn_weights", "L0_ffn_scale", "L0_ffn_bias"]


def build(nc):
    shapes = {"x": [B * T, D], "ctx_1024": [B * T, D], "L0_attn_w_attn": [D, D + 2 * HD], "L0_attn_w_proj": [D, D],
              "L0_xattn_Wq": [D, D], "L0_xattn_Wkv": [D, 2 * D], "L0_xattn_Wproj": [D, D], "L0_xattn_q_gamma": [HD],
              "L0_xattn_k_gamma": [HD], "L0_ffn_weights": [D, D], "L0_ffn_scale": [D], "L0_ffn_bias": [D]}
    ins = [nc.dram_tensor("in_" + n, shapes[n], F32, kind="ExternalInput").ap() for n in _IN]
    out = nc.dram_tensor("out", [B * T, D], F32, kind="ExternalOutput").ap()
    spill = {tag: nc.dram_tensor("spill_" + tag, [D, PARTS * T], BF16, kind="Internal").ap()
             for tag in ("qS", "kX", "qX")}
    decoder_program(nc, *ins, out, spill)


def kernel(**inputs):
    import numpy as np
    import concourse.bacc as bacc
    from concourse.bass_utils import run_bass_kernel_spmd

    nc = bacc.Bacc("TRN2", target_bir_lowering=False, num_devices=1)
    build(nc)
    arrays = {}
    for n in _IN:
        a = np.ascontiguousarray(inputs[n])
        arrays["in_" + n] = a.reshape(-1, a.shape[-1]) if a.ndim == 3 else a
    r = run_bass_kernel_spmd(nc, [arrays], core_ids=[0])
    return r.results[0]["out"].reshape(B, T, D)
```

```python
import concourse.bass as bass
import concourse.mybir as mybir
from contextlib import ExitStack

F32 = mybir.dt.float32
BF16 = mybir.dt.bfloat16
ALU = mybir.AluOpType
ACT = mybir.ActivationFunctionType
AX = mybir.AxisListType

P = 128
B, T, D = 16, 256, 256
H = 16
HD = D // H
TT = T // P
DC = D // P
HC = H // DC
PARTS = 3
Q_SLOTS = (0, 1, 0, 1, 0, 2)
K_SLOTS = (0, 0, 1, 1, 2, 0)
QK_ROWS = len(Q_SLOTS) * HD
ROWS = QK_ROWS + 2
SCALE = HD ** -0.5
LN_EPS = 1e-5
RMS_EPS = 1e-6
CLIP = 100.0
MASKED = -1e30
NBANK = 3

SELF_CHUNKS, CROSS_CHUNKS = 6, 8
MAX_S, MAX_X = 12, 16

LAG = {
    "load_x": -1, "xT": -1, "qS": -1, "kvS": -1, "kS": -1, "vS": -1, "qRest": -1, "qMid": -1, "qLow": -1, "qS3": -1, "maxS": -1, "mS": -1,
    "load_res": 0, "qkS": 0, "pvS": 0, "otS": 0, "t1S": 0, "t2S": 0, "t3S": 0, "stats1": 0, "aggr1": 0, "ln1": 0,
    "load_ctx": 0, "cT": 0, "kv": 0, "kSq": 0, "kSum": 0, "kN": 0, "kX": 0, "kXRest": 0, "kXMid": 0, "kXLow": 0,
    "kX3": 0, "vX": 0,
    "x1T": 0, "q": 0, "qSq": 0, "qSum": 0, "qN": 0, "qX": 0, "qXRest": 0, "qXMid": 0, "qXLow": 0, "qX3": 0,
    "keep": 0, "maxX": 1, "mX": 1, "qkX": 1, "pvX": 1, "otX": 1,
    "t1X": 1, "t2X": 1, "t3X": 1, "stats2": 1, "aggr2": 1,
    "ln2": 2, "x2T": 2, "ffn": 2, "fClip": 2, "fSum": 2, "stats3": 2, "aggr3": 2, "ln3": 2,
}
BANKED = {"wT", "xT", "qS", "kvS", "kS", "maxS", "mS", "t1S", "t2S", "t3S", "cT", "kv", "kX", "x1T", "q", "qX",
          "maxX", "mX", "t1X", "t2X", "t3X", "x2T", "ffn"}

ORDER = """
qkS:0 maxX:0 qkS:1 load_ctx maxX:1 qkS:2 ln2 qkS:3 pvS:0 load_res maxX:2 x2T maxX:3 pvS:1 maxX:4 maxX:5 qkS:4
otS:0 qkS:5 pvS:2 maxX:6 maxX:7 maxX:8 pvS:3 pvS:4 maxX:9 cT maxX:10 pvS:5 otS:1 maxX:11 maxX:12 xT maxX:13
load_x maxX:14 t1S:0 t1S:1 maxX:15 ffn fClip fSum stats3 aggr3 kv:0 mX kv:1 t2S ln3 t3S stats1 aggr1 kSq qS kvS
qkX:0 kS kSum ln1 qRest qLow qkX:1 pvX:0 qMid qkX:2 x1T qS3 qkX:3 pvX:1 qkX:4 kN qSum kXRest q qSq vS kX qkX:5
kXMid pvX:2 qkX:6 vX otX:0 pvX:3 maxS:0 kXLow maxS:1 qN maxS:2 pvX:4 qkX:7 maxS:3 pvX:5 pvX:6 qX qXRest pvX:7
maxS:4 qXLow otX:1 maxS:5 kX3 maxS:6 maxS:7 t1X:0 t1X:1 qX3 qXMid maxS:8 maxS:9 t2X maxS:10 maxS:11 mS keep t3X
stats2 aggr2
"""


def schedule():
    out = []
    for item in ORDER.split():
        step, _, k = item.partition(":")
        out.append((step, int(k or 0), LAG[step]))
    return out


SCHEDULE = schedule()
LOOP_FROM, LOOP_TO = 3, B - 1


def active(i, lag):
    return 0 <= i - lag < B


def bank_uses():
    uses, n = {}, 0
    uses[(-1, "wT", 0)] = n
    n += 1
    for i in range(-1, B + 2):
        for step, k, lag in SCHEDULE:
            if step in BANKED and active(i, lag):
                uses[(i, step, k)] = n
                n += 1
    return uses


BANK_USES = bank_uses()
USES = sum(step in BANKED for step, _, _ in SCHEDULE)
assert USES % NBANK == 0


def plus(i, per, c):
    if isinstance(i, int):
        return i * per + c
    e = i if per == 1 else i * per
    return e + c if c > 0 else e - (-c) if c < 0 else e


def bank_at(i, step, k, back=0):
    if isinstance(i, int):
        n = BANK_USES.get((i - back, step, k))
        return (0, None) if n is None else (n % NBANK, n // NBANK)
    n = BANK_USES[(LOOP_FROM, step, k)]
    return n % NBANK, plus(i, USES // NBANK, n // NBANK - (LOOP_FROM + back) * (USES // NBANK))


SIGNALS = {
    "x_in": 16, "ctx_in": 16, "x_res": 16,
    "qS_high": 1, "qS_mid": 1, "qS_low": 1,
    "kS_high": 1, "kS_mid": 1, "kS_low": 1,
    "qS_spilled": 16, "kX_spilled": 16, "qX_spilled": 16,
    "qS_stacked": 96, "kS_stacked": 96, "qX_stacked": 96, "kX_stacked": 96,
    "maxS_high": 1, "maxX_high": 1, "maxS_stacked": 32, "maxX_stacked": 32,
    "scoresS": SELF_CHUNKS, "expS": SELF_CHUNKS, "maskedS": SELF_CHUNKS, "pvS": 2, "otS": 2,
    "scoresX": CROSS_CHUNKS, "expX": CROSS_CHUNKS, "pvX": 2, "otX": 2,
    "rdenS": 2, "rdenX": 2,
    "vS_placed": 1, "k_sq": 1, "k_ss": 1, "k_ms": 1, "k_rs": 1, "k_norm": 1, "v_placed": 2,
    "q_sq": 1, "q_ss": 1, "q_ms": 1, "q_rs": 1, "q_norm": 1,
    "kX_high": 1, "kX_mid": 1, "kX_low": 1, "qX_high": 1, "qX_mid": 1, "qX_low": 1,
    "ln1_stats": 2, "ln1_aggr": 2, "ln1_var": 1, "ln1_rstd": 1, "x1": 2,
    "ln2_stats": 2, "ln2_aggr": 2, "ln2_var": 1, "ln2_rstd": 1, "x2": 2,
    "ln3_stats": 2, "ln3_aggr": 2, "ln3_var": 1, "ln3_rstd": 1, "x3": 2,
    "x1_kept": 1, "f_clip": 1, "f_sum": 1, "stored": 16,
}


def decoder_program(nc, x, ctx_in_d, w_attn, w_proj, wq, wkv, wproj, q_gamma, k_gamma, ffn_w, ffn_scale, ffn_bias,
                    out, spill):
    es = ExitStack()
    with es:
        def sb(name, shape, dt=F32):
            return es.enter_context(nc.sbuf_tensor(name, shape, dt))

        def pb(name, shape):
            return es.enter_context(nc.psum_tensor(name, shape, F32))

        def sem(name):
            return es.enter_context(nc.semaphore(name))

        ident = sb("ident", [P, P])
        identb = sb("identb", [P, P], BF16)
        causal = sb("causal", [P, 4, P], BF16)
        halfpow = sb("halfpow", [P, TT * H])
        wa = sb("wa", [P, DC, D + 2 * HD])
        wp = sb("wp", [P, DC, D])
        wqx = sb("wqx", [P, DC, D])
        wkvx = sb("wkvx", [P, DC, 2 * D])
        wpx = sb("wpx", [P, DC, D])
        wf_raw = sb("wf_raw", [P, DC, D])
        wf_ge = sb("wf_ge", [P, DC, D])
        wf_sign = sb("wf_sign", [P, DC, D])
        wfT = sb("wfT", [P, DC, D])
        qg = sb("qg", [P, 1])
        kg = sb("kg", [P, 1])
        fscale = sb("fscale", [P, D])
        fbias = sb("fbias", [P, D])
        x_in = sb("x_in", [P, TT, D])
        x_res = sb("x_res", [P, TT, D])
        ctx = sb("ctx", [P, TT, D])
        x1 = sb("x1", [P, TT, D])
        x1_res = sb("x1_res", [P, TT, D])
        x2 = sb("x2", [P, TT, D])
        x3 = sb("x3", [P, TT, D])
        sum1 = sb("sum1", [P, TT, D])
        sum2 = sb("sum2", [P, TT, D])
        f2 = sb("f2", [P, TT, D])
        f3 = sb("f3", [P, TT, D])
        sum3 = sb("sum3", [P, TT, D])
        stats = {n: sb(f"stats{n}", [P, TT, 6]) for n in (1, 2, 3)}
        mv = {n: sb(f"mv{n}", [P, TT, 2]) for n in (1, 2, 3)}
        ve = {n: sb(f"ve{n}", [P, TT]) for n in (1, 2, 3)}
        rstd = {n: sb(f"rstd{n}", [P, TT]) for n in (1, 2, 3)}
        xT = sb("xT", [P, DC, T])
        ctxT = sb("ctxT", [P, DC, T])
        x1T = sb("x1T", [P, DC, T])
        x2T = sb("x2T", [P, DC, T])
        restS = sb("restS", [P, DC, T])
        partS = sb("partS", [P, DC, PARTS, T], BF16)
        kvtok = sb("kvtok", [P, TT, 2 * HD])
        restK = sb("restK", [HD, T])
        partK = sb("partK", [HD, PARTS, T], BF16)
        kvraw = sb("kvraw", [P, TT, 2 * D])
        qraw = sb("qraw", [P, TT, D])
        squares = {"k": sb("k_squares", [P, TT, D]), "q": sb("q_squares", [P, TT, D])}
        ss = {n: sb(n + "_ssum", [P, TT * H]) for n in "kq"}
        ms = {n: sb(n + "_msq", [P, TT * H]) for n in "kq"}
        rs = {n: sb(n + "_rsq", [P, TT * H]) for n in "kq"}
        normed = {n: sb(n + "_normed", [P, TT, D]) for n in "kq"}
        restX = {n: sb(n + "_rest", [P, DC, T]) for n in "kq"}
        partX = {n: sb(n + "_parts", [P, DC, PARTS, T], BF16) for n in "kq"}
        qaS = sb("qaS", [ROWS, H, T], BF16)
        kaS = sb("kaS", [ROWS, T], BF16)
        qaX = sb("qaX", [ROWS, H, T], BF16)
        kaX = sb("kaX", [ROWS, H, T], BF16)
        maxS = sb("maxS", [P, TT, H])
        maxX = sb("maxX", [P, TT, H])
        negS = sb("negS", [H, 2, T], BF16)
        negX = sb("negX", [H, 2, T], BF16)
        ptS0 = sb("ptS0", [P, H, T])
        ptS1 = sb("ptS1", [P, H, P])
        ptX = sb("ptX", [P, TT, H, T])
        vaS = sb("vaS", [P, TT, 2 * HD])
        vaX = sb("vaX", [P, TT, H, 2 * HD])
        ot = {n: sb("ot" + n, [P, 4, T]) for n in "SX"}
        rden = {n: sb("rden" + n, [P, TT, H]) for n in "SX"}
        on = {n: sb("on" + n, [P, TT, D]) for n in "SX"}
        onT = {n: sb("onT" + n, [P, DC, T]) for n in "SX"}

        score = [pb(f"score{j}", [P, 1024]) for j in range(2)]
        out_bank = pb("out_bank", [P, 512])
        work = [pb(f"work{j}", [P, 512]) for j in range(NBANK)]

        filled = [sem(f"work{j}_filled") for j in range(NBANK)]
        drained = [sem(f"work{j}_drained") for j in range(NBANK)]
        signal = {name: sem(name) for name in SIGNALS}
        weights_in = sem("weights_in")
        ones_set = sem("ones_set")
        const_set = sem("const_set")
        sign_set = sem("sign_set")
        passed_dve = sem("passed_dve")
        passed_sp = sem("passed_sp")
        passed_pool = sem("passed_pool")

        def some(i, lag):
            return not isinstance(i, int) or i >= lag

        def count(i, lag, name, k=None):
            per = SIGNALS[name]
            if isinstance(i, int) and i - lag >= B:
                return B * per
            return plus(i, per, (per if k is None else k) - lag * per)

        class Use:

            def __init__(self, bank, before):
                self.bank, self.n = work[bank], before
                self.filled, self.drained = filled[bank], drained[bank]
                self.used = not isinstance(before, int) or before > 0

            def __getitem__(self, at):
                return self.bank[at]

        def use(i, step, k, back=0):
            bank, before = bank_at(i, step, k, back)
            return None if before is None else Use(bank, before)

        def run(eng, steps):
            def iteration(i):
                for step, k, lag in SCHEDULE:
                    if step in steps and (not isinstance(i, int) or active(i, lag)):
                        steps[step](i, k, lag)
            for i in range(-1, LOOP_FROM):
                iteration(i)
            with eng.Fori(LOOP_FROM, LOOP_TO) as i:
                iteration(i)
            for i in range(LOOP_TO, B + 2):
                iteration(i)

        n_weights = 16 * (6 + 2 * HC + 2)
        block = es.enter_context(nc.Block())

        @block.sync
        def _(sp):
            def rows(i, lag):
                return bass.ds(plus(i, T, -lag * T), T) if not isinstance(i, int) else slice((i - lag) * T, (i - lag + 1) * T)

            def tokens(ap, i, lag):
                return ap[rows(i, lag), :].rearrange("(t p) d -> p t d", p=P)

            def load(i, lag, dst, src, name):
                sp.dma_start(dst[:, :, :], tokens(src, i, lag)).then_inc(signal[name], 16)

            sp.dma_start(x_in[:, :, :], tokens(x, 0, 0)).then_inc(signal["x_in"], 16)
            for dst, src in ((wa, w_attn), (wqx, wq), (wkvx, wkv), (wp, w_proj), (wpx, wproj), (wf_raw, ffn_w)):
                sp.dma_start(dst[:, :, :], src.rearrange("(c p) n -> p c n", p=P)).then_inc(weights_in, 16)
            for dst, src in ((qg, q_gamma), (kg, k_gamma)):
                for h in range(HC):
                    sp.dma_start(dst[h * HD:(h + 1) * HD, :], src.rearrange("(d a) -> d a", a=1)).then_inc(weights_in, 16)
            for dst, src in ((fscale, ffn_scale), (fbias, ffn_bias)):
                sp.dma_start(dst[:, :], src.partition_broadcast(P)).then_inc(weights_in, 16)

            def load_x(i, k, lag):
                if not (isinstance(i, int) and i - lag == 0):
                    last = use(i, "xT", 0, back=1)
                    if last:
                        sp.wait_ge(last.filled, last.n + 1)
                        sp.sem_inc(passed_sp, 1)
                    load(i, lag, x_in, x, "x_in")

            def load_ctx(i, k, lag):
                last = use(i, "cT", 0, back=1)
                if last:
                    sp.wait_ge(last.filled, last.n + 1)
                    sp.sem_inc(passed_sp, 1)
                load(i, lag, ctx, ctx_in_d, "ctx_in")

            def load_res(i, k, lag):
                source = use(i, "t3S", 0, back=1)
                if source:
                    sp.wait_ge(source.drained, source.n + 1)
                    sp.sem_inc(passed_sp, 1)
                load(i, lag, x_res, x, "x_res")

            def spilling(tag, parts):
                def emit(i, k, lag):
                    sp.wait_ge(signal[tag + "_low"], count(i, lag, tag + "_low"))
                    sp.sem_inc(passed_sp, 1)
                    if some(i, lag + 1):
                        sp.wait_ge(signal[tag + "_stacked"], count(i, lag + 1, tag + "_stacked"))
                        sp.sem_inc(passed_sp, 1)
                    sp.dma_start(spill[tag].rearrange("(c p) m -> p c m", p=P),
                                 parts[:, :, :, :].rearrange("p c a t -> p c (a t)"))\
                        .then_inc(signal[tag + "_spilled"], 16)
                return emit

            def stacking(tag, slots, dst, scores):
                def emit(i, k, lag):
                    if some(i, lag + 1):
                        sp.wait_ge(signal[scores], count(i, lag + 1, scores))
                        sp.sem_inc(passed_sp, 1)
                    sp.wait_ge(signal[tag + "_spilled"], count(i, lag, tag + "_spilled"))
                    sp.sem_inc(passed_sp, 1)
                    src = spill[tag].rearrange("(h d) (a t) -> d h a t", d=HD, a=PARTS)
                    for s, part in enumerate(slots):
                        sp.dma_start(dst[s * HD:(s + 1) * HD, :, :], src[:, :, part, :])\
                            .then_inc(signal[tag + "_stacked"], 16)
                return emit

            def qS3(i, k, lag):
                sp.wait_ge(signal["kS_low"], count(i, lag, "kS_low"))
                sp.sem_inc(passed_sp, 1)
                if some(i, lag + 1):
                    sp.wait_ge(signal["scoresS"], count(i, lag + 1, "scoresS"))
                    sp.sem_inc(passed_sp, 1)
                for s, part in enumerate(K_SLOTS):
                    sp.dma_start(kaS[s * HD:(s + 1) * HD, :], partK[:, part, :]).then_inc(signal["kS_stacked"], 16)
                stacking("qS", Q_SLOTS, qaS, "scoresS")(i, k, lag)

            def max_rows(i, lag, tag, neg, dst):
                source = use(i, "m" + tag, 0)
                sp.wait_ge(source.drained, source.n + 1)
                sp.sem_inc(passed_sp, 1)
                for part in range(2):
                    sp.dma_start(dst[QK_ROWS + part:QK_ROWS + part + 1, :, :], neg[:, part, :])\
                        .then_inc(signal[f"max{tag}_stacked"], 16)

            def mS(i, k, lag):
                if some(i, lag + 1):
                    sp.wait_ge(signal["scoresS"], count(i, lag + 1, "scoresS"))
                    sp.sem_inc(passed_sp, 1)
                max_rows(i, lag, "S", negS, qaS)

            def mX(i, k, lag):
                if some(i, lag + 1):
                    sp.wait_ge(signal["scoresX"], count(i, lag + 1, "scoresX"))
                    sp.sem_inc(passed_sp, 1)
                max_rows(i, lag, "X", negX, qaX)

            def ln3(i, k, lag):
                sp.wait_ge(signal["x3"], count(i, lag, "x3"))
                sp.sem_inc(passed_sp, 1)
                sp.dma_start(tokens(out, i, lag), x3[:, :, :]).then_inc(signal["stored"], 16)

            run(sp, {"load_x": load_x, "load_ctx": load_ctx, "load_res": load_res, "qLow": spilling("qS", partS),
                     "qS3": qS3, "kXLow": spilling("kX", partX["k"]), "kX3": stacking("kX", K_SLOTS, kaX, "scoresX"),
                     "qXLow": spilling("qX", partX["q"]), "qX3": stacking("qX", Q_SLOTS, qaX, "scoresX"), "mS": mS, "mX": mX, "ln3": ln3})
            sp.wait_ge(signal["stored"], 16 * B)

        @block.tensor
        def _(pe):
            def transpose_tokens(i, step, src):
                w = use(i, step, 0)
                if w.used:
                    pe.wait_ge(w.drained, w.n)
                for c in range(DC):
                    for t in range(TT):
                        mm = pe.transpose(w[:, c * T + t * P:c * T + (t + 1) * P], src[:, t, c * P:(c + 1) * P], ident[:, :])
                mm.then_inc(w.filled, 1)

            def project_tokens(i, step, k, srcT, weights, tile_at):
                w = use(i, step, k)
                if w.used:
                    pe.wait_ge(w.drained, w.n)
                n = weights.shape[2]
                for t, col in tile_at.items():
                    for c in range(DC):
                        mm = pe.matmul(w[:, col:col + n], srcT[:, c, t * P:(t + 1) * P], weights[:, c, :],
                                       start=(c == 0), stop=(c == DC - 1))
                mm.then_inc(w.filled, 1)

            def xT_(i, k, lag):
                pe.wait_ge(signal["x_in"], count(i, lag, "x_in"))
                transpose_tokens(i, "xT", x_in)

            def qS(i, k, lag):
                source = use(i, "xT", 0)
                pe.wait_ge(source.drained, source.n + 1)
                w = use(i, "qS", 0)
                if w.used:
                    pe.wait_ge(w.drained, w.n)
                for m in range(DC):
                    for c in range(DC):
                        mm = pe.matmul(w[:, m * T:(m + 1) * T], wa[:, c, m * P:(m + 1) * P], xT[:, c, :],
                                       start=(c == 0), stop=(c == DC - 1))
                mm.then_inc(w.filled, 1)

            def kvS(i, k, lag):
                source = use(i, "xT", 0)
                pe.wait_ge(source.drained, source.n + 1)
                project_tokens(i, "kvS", 0, xT, wa[:, :, D:D + 2 * HD], {0: 0, 1: 2 * HD})

            def kS(i, k, lag):
                source = use(i, "kvS", 0)
                pe.wait_ge(source.drained, source.n + 1)
                w = use(i, "kS", 0)
                if w.used:
                    pe.wait_ge(w.drained, w.n)
                for t in range(TT):
                    mm = pe.matmul(w[0:HD, t * P:(t + 1) * P], kvtok[:, t, 0:HD], ident[:, :], start=True, stop=True)
                mm.then_inc(w.filled, 1)

            def maxS_(i, u, lag):
                if u == 0:
                    pe.wait_ge(signal["qS_stacked"], count(i, lag, "qS_stacked"))
                    pe.wait_ge(signal["kS_stacked"], count(i, lag, "kS_stacked"))
                w = use(i, "maxS", u)
                if w.used:
                    pe.wait_ge(w.drained, w.n)
                if u < 8:
                    for j in range(2):
                        pe.matmul(w[:, j * T:(j + 1) * T], qaS[0:QK_ROWS, 2 * u + j, P:T], kaS[0:QK_ROWS, :],
                                  start=(j == 0), stop=False, skip_group_check=True)
                    mm = pe.matmul(w[:, :].rearrange("p (h k) -> p h k", h=2)[:, :, P:T], identb[:, :],
                                   causal[:, 0:2, :], start=False, stop=True, skip_group_check=True)
                else:
                    for j in range(4):
                        pe.matmul(w[:, j * P:(j + 1) * P], qaS[0:QK_ROWS, 4 * (u - 8) + j, 0:P], kaS[0:QK_ROWS, 0:P],
                                  start=(j == 0), stop=False, skip_group_check=True)
                    mm = pe.matmul(w[:, :], identb[:, :], causal[:, :, :].rearrange("p h k -> p (h k)"),
                                   start=False, stop=True, skip_group_check=True)
                mm.then_inc(w.filled, 1)

            def maxX_(i, u, lag):
                if u == 0:
                    pe.wait_ge(signal["qX_stacked"], count(i, lag, "qX_stacked"))
                    pe.wait_ge(signal["kX_stacked"], count(i, lag, "kX_stacked"))
                w = use(i, "maxX", u)
                if w.used:
                    pe.wait_ge(w.drained, w.n)
                t, h = u // 8, 2 * (u % 8)
                for j in range(2):
                    mm = pe.matmul(w[:, j * T:(j + 1) * T], qaX[0:QK_ROWS, h + j, t * P:(t + 1) * P],
                                   kaX[0:QK_ROWS, h + j, :], start=True, stop=True)
                mm.then_inc(w.filled, 1)

            def turn_max(i, step, last, src):
                source = use(i, *last)
                pe.wait_ge(source.drained, source.n + 1)
                w = use(i, step, 0)
                if w.used:
                    pe.wait_ge(w.drained, w.n)
                for t in range(TT):
                    mm = pe.matmul(w[0:H, t * P:(t + 1) * P], src[:, t, :], ident[:, :], start=True, stop=True)
                mm.then_inc(w.filled, 1)

            def score_slot(i, lag, tag, other, other_lag, n):
                if n >= 2:
                    pe.wait_ge(signal["exp" + tag], count(i, lag, "exp" + tag, n - 1))
                else:
                    if some(i, other_lag):
                        pe.wait_ge(signal["exp" + other], count(i, other_lag, "exp" + other))
                return score[n % 2]

            def qkS(i, n, lag):
                if n == 0:
                    pe.wait_ge(signal["maxS_stacked"], count(i, lag, "maxS_stacked"))
                s = score_slot(i, lag, "S", "X", lag + 2, n)
                if n % 3 < 2:
                    g = 2 * (n // 3) + n % 3
                    for j in range(2):
                        mm = pe.matmul(s[:, j * 512:(j + 1) * 512], kaS[:, 0:P],
                                       qaS[:, 4 * g + 2 * j:4 * g + 2 * j + 2, :], start=True, stop=True)
                else:
                    h = 8 * (n // 3)
                    for j in range(2):
                        mm = pe.matmul(s[:, j * 512:(j + 1) * 512], kaS[:, P:T],
                                       qaS[:, h + 4 * j:h + 4 * j + 4, P:T], start=True, stop=True)
                mm.then_inc(signal["scoresS"], 1)

            def qkX(i, n, lag):
                if n == 0:
                    pe.wait_ge(signal["maxX_stacked"], count(i, lag, "maxX_stacked"))
                s = score_slot(i, lag, "X", "S", lag - 1, n)
                g, kt = n // 2, n % 2
                for j in range(4):
                    h = 4 * g + j
                    mm = pe.matmul(s[:, j * T:(j + 1) * T], kaX[:, h, kt * P:(kt + 1) * P], qaX[:, h, :],
                                   start=True, stop=True)
                mm.then_inc(signal["scoresX"], 1)

            def pvS(i, n, lag):
                half = n // 3
                pe.wait_ge(signal["maskedS"], count(i, lag, "maskedS", n + 1))
                if n == 0:
                    pe.wait_ge(signal["vS_placed"], count(i, lag, "vS_placed"))
                    if some(i, lag + 2):
                        pe.wait_ge(signal["otX"], count(i, lag + 2, "otX"))
                if n == 3:
                    pe.wait_ge(signal["otS"], count(i, lag, "otS", 1))
                if n % 3 < 2:
                    g = 2 * half + n % 3
                    for j in range(4):
                        pe.matmul(out_bank[32 * j:32 * (j + 1), (n % 3) * T:(n % 3 + 1) * T], vaS[:, 0, :],
                                  ptS0[:, 4 * g + j, :], start=(n % 3 == 0), stop=False, skip_group_check=True)
                else:
                    for gg in range(2):
                        for j in range(4):
                            mm = pe.matmul(out_bank[32 * j:32 * (j + 1), gg * T + P:(gg + 1) * T], vaS[:, 1, :],
                                           ptS1[:, 8 * half + 4 * gg + j, :], start=False, stop=True,
                                           skip_group_check=True)
                    mm.then_inc(signal["pvS"], 1)

            def pvX(i, n, lag):
                g, kt = n // 2, n % 2
                pe.wait_ge(signal["expX"], count(i, lag, "expX", n + 1))
                if n == 0:
                    pe.wait_ge(signal["v_placed"], count(i, lag, "v_placed"))
                    if some(i, lag - 1):
                        pe.wait_ge(signal["otS"], count(i, lag - 1, "otS"))
                if n == 4:
                    pe.wait_ge(signal["otX"], count(i, lag, "otX", 1))
                for j in range(4):
                    h = 4 * g + j
                    mm = pe.matmul(out_bank[32 * j:32 * (j + 1), (g % 2) * T:(g % 2 + 1) * T], vaX[:, kt, h, :],
                                   ptX[:, kt, h, :], start=(kt == 0), stop=(kt == 1), skip_group_check=True)
                if n % 4 == 3:
                    mm.then_inc(signal["pvX"], 1)

            def t1(tag):
                def step(i, t, lag):
                    pe.wait_ge(signal["ot" + tag], count(i, lag, "ot" + tag))
                    w = use(i, "t1" + tag, t)
                    if w.used:
                        pe.wait_ge(w.drained, w.n)
                    for g in range(4):
                        mm = pe.transpose(w[:, g * P:(g + 1) * P], ot[tag][:, g, t * P:(t + 1) * P], ident[:, :])
                    mm.then_inc(w.filled, 1)
                return step

            def t2(tag):
                def step(i, k, lag):
                    source = use(i, "t1" + tag, 1)
                    pe.wait_ge(source.drained, source.n + 1)
                    transpose_tokens(i, "t2" + tag, on[tag])
                return step

            def t3(tag, weights):
                def step(i, k, lag):
                    source = use(i, "t2" + tag, 0)
                    pe.wait_ge(source.drained, source.n + 1)
                    project_tokens(i, "t3" + tag, 0, onT[tag], weights, {0: 0, 1: D})
                return step

            def cT(i, k, lag):
                pe.wait_ge(signal["ctx_in"], count(i, lag, "ctx_in"))
                transpose_tokens(i, "cT", ctx)

            def kv(i, t, lag):
                source = use(i, "cT", 0)
                pe.wait_ge(source.drained, source.n + 1)
                project_tokens(i, "kv", t, ctxT, wkvx, {t: 0})

            def kX(i, k, lag):
                pe.wait_ge(signal["k_norm"], count(i, lag, "k_norm"))
                transpose_tokens(i, "kX", normed["k"])

            def x1T_(i, k, lag):
                pe.wait_ge(signal["x1"], count(i, lag, "x1"))
                transpose_tokens(i, "x1T", x1)

            def q_(i, k, lag):
                source = use(i, "x1T", 0)
                pe.wait_ge(source.drained, source.n + 1)
                project_tokens(i, "q", 0, x1T, wqx, {0: 0, 1: D})

            def qX(i, k, lag):
                pe.wait_ge(signal["q_norm"], count(i, lag, "q_norm"))
                transpose_tokens(i, "qX", normed["q"])

            def x2T_(i, k, lag):
                pe.wait_ge(signal["x2"], count(i, lag, "x2"))
                transpose_tokens(i, "x2T", x2)

            def ffn(i, k, lag):
                source = use(i, "x2T", 0)
                pe.wait_ge(source.drained, source.n + 1)
                project_tokens(i, "ffn", 0, x2T, wfT, {0: 0, 1: D})

            pe.wait_ge(const_set, 5)
            pe.wait_ge(ones_set, 5)
            pe.wait_ge(weights_in, n_weights)
            pe.wait_ge(sign_set, 2)
            for c in range(DC):
                for o in range(DC):
                    mm = pe.transpose(work[0][:, c * D + o * P:c * D + (o + 1) * P], wf_sign[:, o, c * P:(c + 1) * P],
                                      ident[:, :])
            mm.then_inc(filled[0], 1)

            run(pe, {"xT": xT_, "qS": qS, "kvS": kvS, "kS": kS, "maxS": maxS_, "maxX": maxX_,
                     "mS": lambda i, k, lag: turn_max(i, "mS", ("maxS", MAX_S - 1), maxS),
                     "mX": lambda i, k, lag: turn_max(i, "mX", ("maxX", MAX_X - 1), maxX),
                     "qkS": qkS, "qkX": qkX, "pvS": pvS, "pvX": pvX, "t1S": t1("S"), "t1X": t1("X"),
                     "t2S": t2("S"), "t2X": t2("X"), "t3S": t3("S", wp), "t3X": t3("X", wpx), "cT": cT, "kv": kv,
                     "kX": kX, "x1T": x1T_, "q": q_, "qX": qX, "x2T": x2T_, "ffn": ffn})

        @block.scalar
        def _(act):
            def flat(tile):
                return tile[:, :, :].rearrange("p c t -> p (c t)")

            def copy_out(step, dst, product, product_k=0):
                def emit(i, k, lag):
                    last = use(i, product, product_k, back=1)
                    if last:
                        act.wait_ge(last.filled, last.n + 1)
                    w = use(i, step, 0)
                    act.wait_ge(w.filled, w.n + 1)
                    act.activation(flat(dst), w[:, :], ACT.Copy).then_inc(w.drained, 1)
                return emit

            def kv(i, t, lag):
                if some(i, lag + 1):
                    act.wait_ge(signal["k_norm"], count(i, lag + 1, "k_norm"))
                    act.wait_ge(signal["v_placed"], count(i, lag + 1, "v_placed"))
                w = use(i, "kv", t)
                act.wait_ge(w.filled, w.n + 1)
                act.activation(kvraw[:, t, :], w[:, :], ACT.Copy).then_inc(w.drained, 1)

            def q_(i, k, lag):
                if some(i, lag + 1):
                    act.wait_ge(signal["q_norm"], count(i, lag + 1, "q_norm"))
                w = use(i, "q", 0)
                act.wait_ge(w.filled, w.n + 1)
                act.activation(flat(qraw), w[:, :], ACT.Copy).then_inc(w.drained, 1)

            def qS(i, k, lag):
                w = use(i, "qS", 0)
                act.wait_ge(w.filled, w.n + 1)
                if some(i, lag + 1):
                    act.wait_ge(signal["qS_spilled"], count(i, lag + 1, "qS_spilled"))
                act.activation(partS[:, :, 0, :], w[:, :].rearrange("p (c t) -> p c t", c=DC), ACT.Copy)\
                    .then_inc(signal["qS_high"], 1)

            def kS(i, k, lag):
                w = use(i, "kS", 0)
                act.wait_ge(w.filled, w.n + 1)
                if some(i, lag + 1):
                    act.wait_ge(signal["kS_stacked"], count(i, lag + 1, "kS_stacked"))
                act.activation(partK[:, 0, :], w[0:HD, 0:T], ACT.Copy).then_inc(signal["kS_high"], 1)

            def kvS(i, k, lag):
                last = use(i, "kS", 0, back=1)
                if last:
                    act.wait_ge(last.filled, last.n + 1)
                w = use(i, "kvS", 0)
                act.wait_ge(w.filled, w.n + 1)
                act.activation(kvtok[:, :, :].rearrange("p t d -> p (t d)"), w[:, 0:TT * 2 * HD], ACT.Copy)\
                    .then_inc(w.drained, 1)

            def vS(i, k, lag):
                if some(i, lag + 1):
                    act.wait_ge(signal["pvS"], count(i, lag + 1, "pvS"))
                source = use(i, "kvS", 0)
                act.wait_ge(source.drained, source.n + 1)
                act.wait_ge(ones_set, 5)
                act.activation(vaS[:, :, 0:HD], kvtok[:, :, HD:2 * HD], ACT.Copy).then_inc(signal["vS_placed"], 1)

            def qMid(i, k, lag):
                source = use(i, "qS", 0)
                act.wait_ge(source.drained, source.n + 1)
                act.activation(partS[:, :, 1, :], restS[:, :, :], ACT.Copy).then_inc(signal["qS_mid"], 1)
                source = use(i, "kS", 0)
                act.wait_ge(source.drained, source.n + 1)
                act.activation(partK[:, 1, :], restK[:, :], ACT.Copy).then_inc(signal["kS_mid"], 1)

            def neg_high(tag, neg):
                def emit(i, k, lag):
                    w = use(i, "m" + tag, 0)
                    act.wait_ge(w.filled, w.n + 1)
                    if some(i, lag + 1):
                        act.wait_ge(signal[f"max{tag}_stacked"], count(i, lag + 1, f"max{tag}_stacked"))
                    act.activation(neg[:, 0, :], w[0:H, 0:T], ACT.Copy, scale=-1.0)\
                        .then_inc(signal[f"max{tag}_high"], 1)
                return emit

            def expS(i, n, lag):
                act.wait_ge(signal["scoresS"], count(i, lag, "scoresS", n + 1))
                if some(i, lag + 1):
                    act.wait_ge(signal["pvS"], count(i, lag + 1, "pvS", n // 3 + 1))
                if n % 3 < 2:
                    g = 2 * (n // 3) + n % 3
                    dst = ptS0[:, 4 * g:4 * g + 4, :]
                else:
                    dst = ptS1[:, 8 * (n // 3):8 * (n // 3) + 8, :]
                act.activation(dst.rearrange("p h q -> p (h q)"), score[n % 2][:, :], ACT.Exp, scale=SCALE)\
                    .then_inc(signal["expS"], 1)

            def expX(i, n, lag):
                act.wait_ge(signal["scoresX"], count(i, lag, "scoresX", n + 1))
                if some(i, lag + 1):
                    act.wait_ge(signal["pvX"], count(i, lag + 1, "pvX", n // 4 + 1))
                g, kt = n // 2, n % 2
                act.activation(ptX[:, kt, 4 * g:4 * g + 4, :].rearrange("p h q -> p (h q)"), score[n % 2][:, :],
                               ACT.Exp, scale=SCALE).then_inc(signal["expX"], 1)

            def otev(tag):
                def emit(i, half, lag):
                    act.wait_ge(signal["pv" + tag], count(i, lag, "pv" + tag, half + 1))
                    last = use(i, "t1" + tag, 1, back=1)
                    if last:
                        act.wait_ge(last.filled, last.n + 1)
                    act.activation(ot[tag][:, 2 * half:2 * half + 2, :].rearrange("p g t -> p (g t)"), out_bank[:, :],
                                   ACT.Copy).then_inc(signal["ot" + tag], 1)
                return emit

            def square(n, src, step, last_k):
                def emit(i, k, lag):
                    source = use(i, step, last_k)
                    act.wait_ge(source.drained, source.n + 1)
                    if some(i, lag + 1):
                        act.wait_ge(signal[n + "_ss"], count(i, lag + 1, n + "_ss"))
                    act.activation(squares[n][:, :, :], src, ACT.Square).then_inc(signal[n + "_sq"], 1)
                return emit

            def high(n, gamma):
                def emit(i, k, lag):
                    w = use(i, n + "X", 0)
                    act.wait_ge(w.filled, w.n + 1)
                    if some(i, lag + 1):
                        act.wait_ge(signal[n + "X_spilled"], count(i, lag + 1, n + "X_spilled"))
                    act.activation(partX[n][:, :, 0, :], w[:, :].rearrange("p (c t) -> p c t", c=DC), ACT.Copy,
                                   scale=gamma[:, 0:1]).then_inc(signal[n + "X_high"], 1)
                return emit

            def mid(n):
                def emit(i, k, lag):
                    source = use(i, n + "X", 0)
                    act.wait_ge(source.drained, source.n + 1)
                    act.activation(partX[n][:, :, 1, :], restX[n][:, :, :], ACT.Copy).then_inc(signal[n + "X_mid"], 1)
                return emit

            act.wait_ge(weights_in, n_weights)

            run(act, {
                "xT": copy_out("xT", xT, "qS"), "qS": qS, "kvS": kvS, "kS": kS, "vS": vS, "qMid": qMid,
                "cT": copy_out("cT", ctxT, "kv", 1), "kv": kv, "kSq": square("k", kvraw[:, :, 0:D], "kv", 1),
                "kX": high("k", kg), "kXMid": mid("k"), "qX": high("q", qg), "qXMid": mid("q"),
                "x1T": copy_out("x1T", x1T, "q"), "q": q_, "qSq": square("q", qraw[:, :, :], "q", 0),
                "x2T": copy_out("x2T", x2T, "ffn"),
                "t2S": copy_out("t2S", onT["S"], "t3S"), "t2X": copy_out("t2X", onT["X"], "t3X"),
                "mS": neg_high("S", negS), "mX": neg_high("X", negX),
                "qkS": expS, "qkX": expX, "otS": otev("S"), "otX": otev("X"),
            })

        @block.vector
        def _(dve):
            dve.memset(halfpow[:, :], -0.5).then_inc(ones_set, 1)
            dve.memset(kaS[QK_ROWS:ROWS, :], 1.0).then_inc(ones_set, 1)
            dve.memset(kaX[QK_ROWS:ROWS, :, :].rearrange("p h t -> p (h t)"), 1.0).then_inc(ones_set, 1)
            dve.memset(vaS[:, :, :], 1.0).then_inc(ones_set, 1)
            dve.memset(vaX[:, :, :, :].rearrange("p t h d -> p (t h d)"), 1.0).then_inc(ones_set, 1)
            dve.wait_ge(weights_in, n_weights)
            dve.tensor_scalar(wf_ge[:, :, :], wf_raw[:, :, :], 0.0, 2.0, ALU.is_ge, ALU.mult).then_inc(sign_set, 1)
            dve.wait_ge(sign_set, 1)
            dve.tensor_scalar(wf_sign[:, :, :], wf_ge[:, :, :], -1.0, None, ALU.add).then_inc(sign_set, 1)

            dve.wait_ge(filled[0], 1)
            dve.tensor_tensor(wfT[:, :, :], work[0][:, :].rearrange("p (c o) -> p c o", c=DC),
                              fscale[:, :].unsqueeze(1).to_broadcast([P, DC, D]), ALU.mult).then_inc(drained[0], 1)

            def qRest(i, k, lag):
                w = use(i, "qS", 0)
                dve.wait_ge(w.filled, w.n + 1)
                dve.wait_ge(signal["qS_high"], count(i, lag, "qS_high"))
                if some(i, lag + 1):
                    dve.wait_ge(signal["qS_low"], count(i, lag + 1, "qS_low"))
                dve.tensor_tensor(restS[:, :, :], w[:, :].rearrange("p (c t) -> p c t", c=DC), partS[:, :, 0, :],
                                  ALU.subtract).then_inc(w.drained, 1)
                w = use(i, "kS", 0)
                dve.wait_ge(w.filled, w.n + 1)
                dve.wait_ge(signal["kS_high"], count(i, lag, "kS_high"))
                if some(i, lag + 1):
                    dve.wait_ge(signal["kS_low"], count(i, lag + 1, "kS_low"))
                dve.tensor_tensor(restK[:, :], w[0:HD, 0:T], partK[:, 0, :], ALU.subtract).then_inc(w.drained, 1)

            def qLow(i, k, lag):
                dve.wait_ge(signal["qS_mid"], count(i, lag, "qS_mid"))
                dve.tensor_tensor(partS[:, :, 2, :], restS[:, :, :], partS[:, :, 1, :], ALU.subtract)\
                    .then_inc(signal["qS_low"], 1)
                dve.wait_ge(signal["kS_mid"], count(i, lag, "kS_mid"))
                dve.tensor_tensor(partK[:, 2, :], restK[:, :], partK[:, 1, :], ALU.subtract)\
                    .then_inc(signal["kS_low"], 1)

            def maxS_(i, u, lag):
                if u == 0:
                    last = use(i, "mS", 0, back=1)
                    if last:
                        dve.wait_ge(last.filled, last.n + 1)
                w = use(i, "maxS", u)
                dve.wait_ge(w.filled, w.n + 1)
                if u < 8:
                    dve.tensor_reduce(maxS[:, 1, 2 * u:2 * u + 2], w[:, :].rearrange("p (h k) -> p h k", h=2), AX.X,
                                      ALU.max).then_inc(w.drained, 1)
                else:
                    dve.tensor_reduce(maxS[:, 0, 4 * (u - 8):4 * (u - 8) + 4], w[:, :].rearrange("p (h k) -> p h k", h=4),
                                      AX.X, ALU.max).then_inc(w.drained, 1)

            def maxX_(i, u, lag):
                if u == 0:
                    last = use(i, "mX", 0, back=1)
                    if last:
                        dve.wait_ge(last.filled, last.n + 1)
                w = use(i, "maxX", u)
                dve.wait_ge(w.filled, w.n + 1)
                t, h = u // 8, 2 * (u % 8)
                dve.tensor_reduce(maxX[:, t, h:h + 2], w[:, :].rearrange("p (h k) -> p h k", h=2), AX.X, ALU.max)\
                    .then_inc(w.drained, 1)

            def neg_low(tag, neg):
                def emit(i, k, lag):
                    w = use(i, "m" + tag, 0)
                    dve.wait_ge(w.filled, w.n + 1)
                    dve.wait_ge(signal[f"max{tag}_high"], count(i, lag, f"max{tag}_high"))
                    if some(i, lag + 1):
                        dve.wait_ge(signal[f"max{tag}_stacked"], count(i, lag + 1, f"max{tag}_stacked"))
                    dve.scalar_tensor_tensor(neg[:, 1, :], w[0:H, 0:T], -1.0, neg[:, 0, :], ALU.mult, ALU.subtract)\
                        .then_inc(w.drained, 1)
                return emit

            def normalise(tag):
                def emit(i, t, lag):
                    w = use(i, "t1" + tag, t)
                    dve.wait_ge(w.filled, w.n + 1)
                    last = use(i, "t2" + tag, 0, back=1)
                    if last:
                        dve.wait_ge(last.filled, last.n + 1)
                    o = w[:, :].rearrange("p (h e) -> p h e", e=2 * HD)
                    dve.reciprocal(rden[tag][:, t, :], o[:, :, HD]).then_inc(signal["rden" + tag], 1)
                    dve.wait_ge(signal["rden" + tag], count(i, lag, "rden" + tag, t + 1))
                    dve.tensor_tensor(on[tag][:, t, :].rearrange("p (h d) -> p h d", d=HD), o[:, :, 0:HD],
                                      rden[tag][:, t, :].unsqueeze(2).to_broadcast([P, H, HD]), ALU.mult)\
                        .then_inc(w.drained, 1)
                return emit

            def moments(n, src, summed):
                def stat(i, k, lag):
                    summed(i, lag)
                    for t in range(TT):
                        dve.bn_stats(stats[n][:, t, :], src[:, t, :]).then_inc(signal[f"ln{n}_stats"], 1)

                def aggr(i, k, lag):
                    for t in range(TT):
                        dve.wait_ge(signal[f"ln{n}_stats"], count(i, lag, f"ln{n}_stats", t + 1))
                        dve.sem_inc(passed_dve, 1)
                        dve.bn_aggr(mv[n][:, t, :], stats[n][:, t, :]).then_inc(signal[f"ln{n}_aggr"], 1)
                return stat, aggr

            def residual(tag, n, total, res, res_ready):
                def emit(i, k, lag):
                    w = use(i, "t3" + tag, 0)
                    dve.wait_ge(w.filled, w.n + 1)
                    dve.wait_ge(signal[res_ready], count(i, lag, res_ready))
                    if some(i, lag + 1):
                        dve.wait_ge(signal[f"x{n}"], count(i, lag + 1, f"x{n}"))
                    dve.tensor_tensor(total[:, :, :].rearrange("p t d -> p (t d)"), w[:, :],
                                      res[:, :, :].rearrange("p t d -> p (t d)"), ALU.add).then_inc(w.drained, 1)
                return emit

            def sum1_there(i, lag):
                w = use(i, "t3S", 0)
                dve.wait_ge(w.drained, w.n + 1)

            def sum2_there(i, lag):
                w = use(i, "t3X", 0)
                dve.wait_ge(w.drained, w.n + 1)

            def sum3_there(i, lag):
                dve.wait_ge(signal["f_sum"], count(i, lag, "f_sum"))

            stats1, aggr1 = moments(1, sum1, sum1_there)
            stats2, aggr2 = moments(2, sum2, sum2_there)
            stats3, aggr3 = moments(3, sum3, sum3_there)

            def apply_norm(i, lag, n, src, dst):
                dve.wait_ge(signal[f"ln{n}_rstd"], count(i, lag, f"ln{n}_rstd"))
                for t in range(TT):
                    dve.tensor_scalar(dst[:, t, :], src[:, t, :], mv[n][:, t, 0:1], rstd[n][:, t:t + 1],
                                      ALU.subtract, ALU.mult).then_inc(signal[f"x{n}"], 1)

            def ln1(i, k, lag):
                if some(i, lag + 1):
                    dve.wait_ge(signal["x1_kept"], count(i, lag + 1, "x1_kept"))
                last = use(i, "x1T", 0, back=1)
                if last:
                    dve.wait_ge(last.filled, last.n + 1)
                apply_norm(i, lag, 1, sum1, x1)

            def ln2(i, k, lag):
                if some(i, lag + 1):
                    dve.wait_ge(signal["f_sum"], count(i, lag + 1, "f_sum"))
                apply_norm(i, lag, 2, sum2, x2)

            def ln3(i, k, lag):
                if some(i, lag + 1):
                    dve.wait_ge(signal["stored"], count(i, lag + 1, "stored"))
                apply_norm(i, lag, 3, sum3, x3)

            def sum_squares(n):
                def emit(i, k, lag):
                    dve.wait_ge(signal[n + "_sq"], count(i, lag, n + "_sq"))
                    if some(i, lag + 1):
                        dve.wait_ge(signal[n + "_ms"], count(i, lag + 1, n + "_ms"))
                    dve.tensor_reduce(ss[n][:, :], squares[n][:, :, :].rearrange("p t (h d) -> p (t h) d", d=HD), AX.X,
                                      ALU.add).then_inc(signal[n + "_ss"], 1)
                return emit

            def rms(n, src, step):
                def emit(i, k, lag):
                    dve.wait_ge(signal[n + "_rs"], count(i, lag, n + "_rs"))
                    last = use(i, step, 0, back=1)
                    if last:
                        dve.wait_ge(last.filled, last.n + 1)
                    dve.tensor_tensor(normed[n][:, :, :].rearrange("p t (h d) -> p t h d", d=HD),
                                      src.rearrange("p t (h d) -> p t h d", d=HD),
                                      rs[n][:, :].rearrange("p (t h) -> p t h", t=TT).unsqueeze(3)
                                      .to_broadcast([P, TT, H, HD]), ALU.mult).then_inc(signal[n + "_norm"], 1)
                return emit

            def rest(n, gamma):
                def emit(i, k, lag):
                    w = use(i, n + "X", 0)
                    dve.wait_ge(w.filled, w.n + 1)
                    dve.wait_ge(signal[n + "X_high"], count(i, lag, n + "X_high"))
                    if some(i, lag + 1):
                        dve.wait_ge(signal[n + "X_low"], count(i, lag + 1, n + "X_low"))
                    dve.scalar_tensor_tensor(restX[n][:, :, :], w[:, :].rearrange("p (c t) -> p c t", c=DC),
                                             gamma[:, 0:1], partX[n][:, :, 0, :], ALU.mult, ALU.subtract)\
                        .then_inc(w.drained, 1)
                return emit

            def low(n):
                def emit(i, k, lag):
                    dve.wait_ge(signal[n + "X_mid"], count(i, lag, n + "X_mid"))
                    dve.tensor_tensor(partX[n][:, :, 2, :], restX[n][:, :, :], partX[n][:, :, 1, :], ALU.subtract)\
                        .then_inc(signal[n + "X_low"], 1)
                return emit

            def ffn(i, k, lag):
                w = use(i, "ffn", 0)
                dve.wait_ge(w.filled, w.n + 1)
                if some(i, lag + 1):
                    dve.wait_ge(signal["f_clip"], count(i, lag + 1, "f_clip"))
                dve.tensor_tensor(f2[:, :, :], w[:, :].rearrange("p (t d) -> p t d", t=TT),
                                  fbias[:, :].unsqueeze(1).to_broadcast([P, TT, D]), ALU.add).then_inc(w.drained, 1)

            def f_clip(i, k, lag):
                source = use(i, "ffn", 0)
                dve.wait_ge(source.drained, source.n + 1)
                if some(i, lag + 1):
                    dve.wait_ge(signal["f_sum"], count(i, lag + 1, "f_sum"))
                dve.tensor_scalar(f3[:, :, :], f2[:, :, :], -CLIP, CLIP, ALU.max, ALU.min).then_inc(signal["f_clip"], 1)

            def f_sum(i, k, lag):
                dve.wait_ge(signal["f_clip"], count(i, lag, "f_clip"))
                if some(i, lag + 1):
                    dve.wait_ge(signal["x3"], count(i, lag + 1, "x3"))
                dve.tensor_tensor(sum3[:, :, :], f3[:, :, :], x2[:, :, :], ALU.add).then_inc(signal["f_sum"], 1)

            run(dve, {
                "qRest": qRest, "qLow": qLow, "maxS": maxS_, "maxX": maxX_,
                "mS": neg_low("S", negS), "mX": neg_low("X", negX), "t1S": normalise("S"), "t1X": normalise("X"),
                "t3S": residual("S", 1, sum1, x_res, "x_res"), "t3X": residual("X", 2, sum2, x1_res, "x1_kept"),
                "ln1": ln1, "ln2": ln2, "ln3": ln3, "kSum": sum_squares("k"), "qSum": sum_squares("q"),
                "kN": rms("k", kvraw[:, :, 0:D], "kX"), "qN": rms("q", qraw[:, :, :], "qX"),
                "kXRest": rest("k", kg), "qXRest": rest("q", qg), "kXLow": low("k"), "qXLow": low("q"), "ffn": ffn,
                "fClip": f_clip, "fSum": f_sum, "stats1": stats1, "aggr1": aggr1, "stats2": stats2, "aggr2": aggr2,
                "stats3": stats3, "aggr3": aggr3,
            })

        @block.gpsimd
        def _(pool):
            def gate():
                pool.sem_inc(passed_pool, 1)

            pool.wait_ge(ones_set, 5)
            pool.memset(ident[:, :], 0.0).then_inc(const_set, 1)
            pool.wait_ge(const_set, 1)
            pool.affine_select(out=ident[:, :], in_=ident[:, :], compare_op=ALU.not_equal, fill=1.0, base=0,
                               pattern=[[-1, P]], channel_multiplier=1).then_inc(const_set, 1)
            pool.wait_ge(const_set, 2)
            pool.tensor_copy(identb[:, :], ident[:, :]).then_inc(const_set, 1)
            pool.memset(causal[:, :, :], 0.0).then_inc(const_set, 1)
            pool.wait_ge(const_set, 4)
            pool.affine_select(out=causal[:, :, :], in_=causal[:, :, :], compare_op=ALU.is_ge, fill=MASKED, base=0,
                               pattern=[[0, 4], [-1, P]], channel_multiplier=1).then_inc(const_set, 1)

            def mask(i, n, lag):
                pool.wait_ge(signal["expS"], count(i, lag, "expS", n + 1))
                gate()
                if n % 3 < 2:
                    g = 2 * (n // 3) + n % 3
                    pt, heads = ptS0[:, 4 * g:4 * g + 4, 0:P], 4
                else:
                    pt, heads = ptS1[:, 8 * (n // 3):8 * (n // 3) + 8, :], 8
                pool.affine_select(out=pt, in_=pt, compare_op=ALU.is_ge, fill=0.0, base=0,
                                   pattern=[[0, heads], [1, P]], channel_multiplier=-1).then_inc(signal["maskedS"], 1)

            def inverse_root(i, lag, n):
                pool.wait_ge(signal[n + "_ss"], count(i, lag, n + "_ss"))
                if some(i, lag + 1):
                    pool.wait_ge(signal[n + "_rs"], count(i, lag + 1, n + "_rs"))
                gate()
                pool.tensor_scalar(ms[n][:, :], ss[n][:, :], 1.0 / HD, RMS_EPS, ALU.mult, ALU.add)\
                    .then_inc(signal[n + "_ms"], 1)
                if some(i, lag + 1):
                    pool.wait_ge(signal[n + "_norm"], count(i, lag + 1, n + "_norm"))
                pool.wait_ge(signal[n + "_ms"], count(i, lag, n + "_ms"))
                pool.tensor_tensor(rs[n][:, :], ms[n][:, :], halfpow[:, :], ALU.pow).then_inc(signal[n + "_rs"], 1)

            def kn(i, k, lag):
                inverse_root(i, lag, "k")

            def place_v(i, k, lag):
                if some(i, lag + 1):
                    pool.wait_ge(signal["pvX"], count(i, lag + 1, "pvX"))
                source = use(i, "kv", 1)
                pool.wait_ge(source.drained, source.n + 1)
                for t in range(TT):
                    gate()
                    pool.tensor_copy(vaX[:, t, :, 0:HD], kvraw[:, t, D:2 * D].rearrange("p (h d) -> p h d", d=HD))\
                        .then_inc(signal["v_placed"], 1)

            def rstd_of(n):
                def emit(i, lag):
                    pool.wait_ge(signal[f"ln{n}_aggr"], count(i, lag, f"ln{n}_aggr"))
                    if some(i, lag + 1):
                        pool.wait_ge(signal[f"ln{n}_rstd"], count(i, lag + 1, f"ln{n}_rstd"))
                    gate()
                    pool.tensor_scalar(ve[n][:, :], mv[n][:, :, 1], LN_EPS, None, ALU.add)\
                        .then_inc(signal[f"ln{n}_var"], 1)
                    if some(i, lag + 1):
                        pool.wait_ge(signal["x%d" % n], count(i, lag + 1, "x%d" % n))
                    pool.wait_ge(signal[f"ln{n}_var"], count(i, lag, f"ln{n}_var"))
                    pool.tensor_tensor(rstd[n][:, :], ve[n][:, :], halfpow[:, 0:TT], ALU.pow)\
                        .then_inc(signal[f"ln{n}_rstd"], 1)
                return emit

            def keep_x1(i, lag):
                pool.wait_ge(signal["x1"], count(i, lag, "x1"))
                source = use(i, "t3X", 0)
                if source:
                    pool.wait_ge(source.drained, source.n + 1)
                gate()
                pool.tensor_copy(x1_res[:, :, :], x1[:, :, :]).then_inc(signal["x1_kept"], 1)

            run(pool, {
                "qkS": mask, "aggr1": lambda i, k, lag: rstd_of(1)(i, lag), "kSum": kn,
                "qSum": lambda i, k, lag: inverse_root(i, lag, "q"),
                "vX": place_v,
                "aggr2": lambda i, k, lag: rstd_of(2)(i, lag),
                "aggr3": lambda i, k, lag: rstd_of(3)(i, lag),
                "keep": lambda i, k, lag: keep_x1(i, lag),
            })


_IN = ["x", "ctx_1024", "L0_attn_w_attn", "L0_attn_w_proj", "L0_xattn_Wq", "L0_xattn_Wkv", "L0_xattn_Wproj",
       "L0_xattn_q_gamma", "L0_xattn_k_gamma", "L0_ffn_weights", "L0_ffn_scale", "L0_ffn_bias"]


def build(nc):
    shapes = {"x": [B * T, D], "ctx_1024": [B * T, D], "L0_attn_w_attn": [D, D + 2 * HD], "L0_attn_w_proj": [D, D],
              "L0_xattn_Wq": [D, D], "L0_xattn_Wkv": [D, 2 * D], "L0_xattn_Wproj": [D, D], "L0_xattn_q_gamma": [HD],
              "L0_xattn_k_gamma": [HD], "L0_ffn_weights": [D, D], "L0_ffn_scale": [D], "L0_ffn_bias": [D]}
    ins = [nc.dram_tensor("in_" + n, shapes[n], F32, kind="ExternalInput").ap() for n in _IN]
    out = nc.dram_tensor("out", [B * T, D], F32, kind="ExternalOutput").ap()
    spill = {tag: nc.dram_tensor("spill_" + tag, [D, PARTS * T], BF16, kind="Internal").ap()
             for tag in ("qS", "kX", "qX")}
    decoder_program(nc, *ins, out, spill)


def kernel(**inputs):
    import numpy as np
    import concourse.bacc as bacc
    from concourse.bass_utils import run_bass_kernel_spmd

    nc = bacc.Bacc("TRN2", target_bir_lowering=False, num_devices=1)
    build(nc)
    arrays = {}
    for n in _IN:
        a = np.ascontiguousarray(inputs[n])
        arrays["in_" + n] = a.reshape(-1, a.shape[-1]) if a.ndim == 3 else a
    r = run_bass_kernel_spmd(nc, [arrays], core_ids=[0])
    return r.results[0]["out"].reshape(B, T, D)
```

```python
import concourse.bass as bass
import concourse.mybir as mybir
from contextlib import ExitStack

F32 = mybir.dt.float32
BF16 = mybir.dt.bfloat16
ALU = mybir.AluOpType
ACT = mybir.ActivationFunctionType
AX = mybir.AxisListType

P = 128
B, T, D = 16, 256, 256
H = 16
HD = D // H
TT = T // P
DC = D // P
HC = H // DC
PARTS = 3
SLOTS = 6
Q_RUNS = ((0, 0, 3), (3, 0, 2), (5, 0, 1))
K_RUNS = ((0, 0, 1), (1, 0, 1), (2, 0, 2), (4, 1, 2))
K_PART1, K_PART2 = 3 * HD, 5 * HD
QK_ROWS = SLOTS * HD
ROWS = QK_ROWS + 2
SCALE = HD ** -0.5
LN_EPS = 1e-5
RMS_EPS = 1e-6
CLIP = 100.0
MASKED = -1e30
NRING = 3
HELD = NRING
NSCORE = 3

SELF_CHUNKS, CROSS_CHUNKS = 12, 16
SELF_GROUPS, CROSS_GROUPS = 6, 8
MAX_S, MAX_X = 12, 16

LAG = {
    "load_x": -1, "xT": -1, "qS": -1, "kvS": -1, "kS": -1, "vS": -1, "qRest": -1, "qMid": -1, "qLow": -1,
    "kLow": -1, "qS3": -1, "maxS": -1, "mS": -1,
    "load_res": 0, "qkS": 0, "pvS": 0, "otS": 0, "t1S": 0, "t2S": 0, "t3S": 0, "stats1": 0, "aggr1": 0, "ln1": 0,
    "load_ctx": 0, "cT": 0, "kv": 0, "kSq": 0, "kSum": 0, "kN": 0, "kX": 0, "kXRest": 0, "kXMid": 0, "kXLow": 0,
    "kX3": 0, "vX": 0,
    "x1T": 0, "q": 0, "qSq": 0, "qSum": 0, "qN": 0, "qX": 0, "qXRest": 0, "qXMid": 0, "qXLow": 0, "qX3": 0,
    "keep": 0, "maxX": 1, "mX": 1, "qkX": 1, "pvX": 1, "otX": 1,
    "t1X": 1, "t2X": 1, "t3X": 1, "stats2": 1, "aggr2": 1,
    "ln2": 2, "x2T": 2, "ffn": 2, "fClip": 2, "fSum": 2, "stats3": 2, "aggr3": 2, "ln3": 2,
}
BANKED = {"wT", "xT", "qS", "kvS", "kS", "maxS", "mS", "t1S", "t2S", "t3S", "cT", "kv", "kX", "x1T", "q", "qX",
          "maxX", "mX", "t1X", "t2X", "t3X", "x2T", "ffn"}
HELD_STEPS = ("qS", "kX", "qX")

ORDER = """
maxX:0 qkS:0 maxX:1 load_res qkS:1 load_x maxX:2 qkS:2 qkS:3 maxX:3 maxX:4 qkS:4 qkS:5 pvS:0 ln2 qkS:6 maxX:5
qkS:7 maxX:6 pvS:1 qkS:8 x2T qkS:9 load_ctx maxX:7 pvS:2 maxX:8 otS:0 qkS:10 qkS:11 maxX:9 xT cT maxX:10 pvS:3
maxX:11 maxX:12 pvS:4 maxX:13 pvS:5 maxX:14 maxX:15 t1S:0 otS:1 t1S:1 kv:0 mX ffn fClip t2S fSum kv:1 stats3 t3S
kvS qkX:0 stats1 qkX:1 aggr1 kSq qkX:2 qS aggr3 qkX:3 kSum ln1 kS qRest pvX:0 qMid qkX:4 qLow kLow x1T qkX:5 ln3
pvX:1 q qkX:6 qSq qkX:7 qkX:8 qSum qkX:9 pvX:2 qkX:10 vX qkX:11 kN otX:0 qkX:12 kX pvX:3 qkX:13 maxS:0 pvX:4
maxS:1 maxS:2 qkX:14 qS3 vS qkX:15 maxS:3 pvX:5 keep kXRest qN pvX:6 maxS:4 kXMid otX:1 kXLow pvX:7 maxS:5
qXRest maxS:6 qX t1X:0 qXLow maxS:7 kX3 maxS:8 maxS:9 maxS:10 t1X:1 qXMid maxS:11 t2X qX3 mS t3X stats2 aggr2
"""


def schedule():
    out = []
    for item in ORDER.split():
        step, _, k = item.partition(":")
        out.append((step, int(k or 0), LAG[step]))
    return out


SCHEDULE = schedule()
LOOP_FROM, LOOP_TO = 3, B - 1


def active(i, lag):
    return 0 <= i - lag < B


def bank_uses():
    uses, ring, held = {}, 0, 0
    for i in range(-1, B + 2):
        if i == 0:
            uses[(0, "wT", 0)] = (ring % NRING, ring // NRING)
            ring += 1
        for step, k, lag in SCHEDULE:
            if step in BANKED and active(i, lag):
                if step in HELD_STEPS:
                    uses[(i, step, k)] = (HELD, held)
                    held += 1
                else:
                    uses[(i, step, k)] = (ring % NRING, ring // NRING)
                    ring += 1
    return uses


BANK_USES = bank_uses()
RING_USES = sum(step in BANKED and step not in HELD_STEPS for step, _, _ in SCHEDULE)
assert RING_USES % NRING == 0
PER_BANK = [RING_USES // NRING] * NRING + [len(HELD_STEPS)]


def plus(i, per, c):
    if isinstance(i, int):
        return i * per + c
    e = i if per == 1 else i * per
    return e + c if c > 0 else e - (-c) if c < 0 else e


def bank_at(i, step, k, back=0):
    if isinstance(i, int):
        return BANK_USES.get((i - back, step, k), (0, None))
    bank, before = BANK_USES[(LOOP_FROM, step, k)]
    return bank, plus(i, PER_BANK[bank], before - (LOOP_FROM + back) * PER_BANK[bank])


SIGNALS = {
    "x_in": 16, "ctx_in": 16, "x_res": 16,
    "qS_high": 1, "qS_mid": 1, "qS_low": 1,
    "kS_high": 1, "kS_mid": 1, "kS_low": 1,
    "qS_spilled": 16, "kX_spilled": 16, "qX_spilled": 16,
    "qS_stacked": 16 * len(Q_RUNS), "qX_stacked": 16 * len(Q_RUNS), "kX_stacked": 16 * len(K_RUNS),
    "maxS_high": 1, "maxX_high": 1, "maxS_stacked": 32, "maxX_stacked": 32,
    "scoresS": SELF_CHUNKS, "expS": SELF_CHUNKS, "maskedS": SELF_GROUPS, "pvS": 2, "otS": 2,
    "scoresX": CROSS_CHUNKS, "expX": CROSS_CHUNKS, "pvX": 2, "otX": 2,
    "rdenS": 2, "rdenX": 2,
    "k_tok": 1, "vS_placed": 1, "k_sq": 1, "k_ss": 1, "k_ms": 1, "k_rs": 1, "k_norm": 1, "v_placed": 2,
    "q_sq": 1, "q_ss": 1, "q_ms": 1, "q_rs": 1, "q_norm": 1,
    "kX_high": DC, "kX_rest": DC - 1, "kX_mid": 1, "kX_low": 1, "qX_high": 1, "qX_mid": 1, "qX_low": 1,
    "ln1_stats": 2, "ln1_aggr": 2, "ln1_var": 1, "ln1_rstd": 1, "x1": 2,
    "ln2_stats": 2, "ln2_aggr": 2, "ln2_var": 1, "ln2_rstd": 1, "x2": 2,
    "ln3_stats": 2, "ln3_aggr": 2, "ln3_var": 1, "ln3_rstd": 1, "x3": 2,
    "x1_kept": 1, "f_clip": 1, "f_sum": 1, "stored": 16,
}


def decoder_program(nc, x, ctx_in_d, w_attn, w_proj, wq, wkv, wproj, q_gamma, k_gamma, ffn_w, ffn_scale, ffn_bias,
                    out, spill):
    es = ExitStack()
    with es:
        def sb(name, shape, dt=F32):
            return es.enter_context(nc.sbuf_tensor(name, shape, dt))

        def pb(name, shape):
            return es.enter_context(nc.psum_tensor(name, shape, F32))

        def sem(name):
            return es.enter_context(nc.semaphore(name))

        ident = sb("ident", [P, P])
        identb = sb("identb", [P, P], BF16)
        causal = sb("causal", [P, 4, P], BF16)
        halfpow = sb("halfpow", [P, TT * H])
        wa = sb("wa", [P, DC, D + 2 * HD])
        waq = sb("waq", [P, DC, D])
        wp = sb("wp", [P, DC, D])
        wqx = sb("wqx", [P, DC, D])
        wkvx = sb("wkvx", [P, DC, 2 * D])
        wpx = sb("wpx", [P, DC, D])
        wf_raw = sb("wf_raw", [P, DC, D])
        wf_ge = sb("wf_ge", [P, DC, D])
        wf_sign = sb("wf_sign", [P, DC, D])
        wfT = sb("wfT", [P, DC, D])
        qg = sb("qg", [P, DC])
        kg = sb("kg", [P, DC])
        gamma = sb("gamma", [P, DC])
        kdrop = sb("kdrop", [QK_ROWS, 2])
        fscale = sb("fscale", [P, D])
        fbias = sb("fbias", [P, D])
        x_in = sb("x_in", [P, TT, D])
        x_res = sb("x_res", [P, TT, D])
        ctx = sb("ctx", [P, TT, D])
        x1 = sb("x1", [P, TT, D])
        x1_res = sb("x1_res", [P, TT, D])
        x2 = sb("x2", [P, TT, D])
        x3 = sb("x3", [P, TT, D])
        sum1 = sb("sum1", [P, TT, D])
        sum2 = sb("sum2", [P, TT, D])
        biased = sb("biased", [P, TT, D])
        clipped = sb("clipped", [P, TT, D])
        sum3 = sb("sum3", [P, TT, D])
        stats = {n: sb(f"stats{n}", [P, TT, 6]) for n in (1, 2, 3)}
        mv = {n: sb(f"mv{n}", [P, TT, 2]) for n in (1, 2, 3)}
        ve = {n: sb(f"ve{n}", [P, TT]) for n in (1, 2, 3)}
        rstd = {n: sb(f"rstd{n}", [P, TT]) for n in (1, 2, 3)}
        xT = sb("xT", [P, DC, T])
        ctxT = sb("ctxT", [P, DC, T])
        x1T = sb("x1T", [P, DC, T])
        x2T = sb("x2T", [P, DC, T])
        restS = sb("restS", [P, DC, T])
        partS = sb("partS", [P, PARTS, DC, T], BF16)
        ktok = sb("ktok", [P, TT, SLOTS, HD])
        vtok = sb("vtok", [P, TT, HD])
        restK = sb("restK", [QK_ROWS, T])
        highK = sb("highK", [QK_ROWS, T], BF16)
        midK = sb("midK", [QK_ROWS, T], BF16)
        kvraw = sb("kvraw", [P, TT, 2 * D])
        qraw = sb("qraw", [P, TT, D])
        squares = {"k": sb("k_squares", [P, TT, D]), "q": sb("q_squares", [P, TT, D])}
        ss = {n: sb(n + "_ssum", [P, TT * H]) for n in "kq"}
        ms = {n: sb(n + "_msq", [P, TT * H]) for n in "kq"}
        rs = {n: sb(n + "_rsq", [P, TT * H]) for n in "kq"}
        normed = {n: sb(n + "_normed", [P, TT, D]) for n in "kq"}
        restX = {n: sb(n + "_rest", [P, DC, T]) for n in "kq"}
        partX = {n: sb(n + "_parts", [P, PARTS, DC, T], BF16) for n in "kq"}
        qaS = sb("qaS", [ROWS, H, T], BF16)
        kaS = sb("kaS", [ROWS, T], BF16)
        qaX = sb("qaX", [ROWS, H, T], BF16)
        kaX = sb("kaX", [ROWS, H, T], BF16)
        maxS = sb("maxS", [P, TT, H])
        maxX = sb("maxX", [P, TT, H])
        negS = sb("negS", [H, 2, T], BF16)
        negX = sb("negX", [H, 2, T], BF16)
        ptS0 = sb("ptS0", [P, H, T])
        ptS1 = sb("ptS1", [P, H, P])
        ptX = sb("ptX", [P, TT, H, T])
        vaS = sb("vaS", [P, TT, 2 * HD])
        vaX = sb("vaX", [P, TT, H, 2 * HD])
        ot = {n: sb("ot" + n, [P, 4, T]) for n in "SX"}
        rden = {n: sb("rden" + n, [P, TT, H]) for n in "SX"}
        on = {n: sb("on" + n, [P, TT, D]) for n in "SX"}
        onT = {n: sb("onT" + n, [P, DC, T]) for n in "SX"}

        score = [pb(f"score{j}", [P, 512]) for j in range(NSCORE)]
        out_bank = pb("out_bank", [P, 512])
        work = [pb(f"work{j}", [P, 512]) for j in range(NRING + 1)]

        filled = [sem(f"work{j}_filled") for j in range(NRING + 1)]
        drained = [sem(f"work{j}_drained") for j in range(NRING + 1)]
        signal = {name: sem(name) for name in SIGNALS}
        wa_in = sem("wa_in")
        weights_in = sem("weights_in")
        ones_set = sem("ones_set")
        const_set = sem("const_set")
        sign_set = sem("sign_set")
        gamma_set = sem("gamma_set")
        waq_set = sem("waq_set")
        passed_dve = sem("passed_dve")
        passed_sp = sem("passed_sp")
        passed_pool = sem("passed_pool")

        def some(i, lag):
            return not isinstance(i, int) or i >= lag

        def count(i, lag, name, k=None):
            per = SIGNALS[name]
            if isinstance(i, int) and i - lag >= B:
                return B * per
            return plus(i, per, (per if k is None else k) - lag * per)

        class Use:

            def __init__(self, bank, before):
                self.bank, self.n = work[bank], before
                self.filled, self.drained = filled[bank], drained[bank]
                self.used = not isinstance(before, int) or before > 0

            def __getitem__(self, at):
                return self.bank[at]

        def use(i, step, k, back=0):
            bank, before = bank_at(i, step, k, back)
            return None if before is None else Use(bank, before)

        def run(eng, steps, set_up=None):
            def iteration(i):
                for step, k, lag in SCHEDULE:
                    if step in steps and (not isinstance(i, int) or active(i, lag)):
                        steps[step](i, k, lag)
            iteration(-1)
            if set_up:
                set_up()
            for i in range(LOOP_FROM):
                iteration(i)
            with eng.Fori(0, (LOOP_TO - LOOP_FROM) // 2) as pair:
                iteration(pair * 2 + LOOP_FROM)
                iteration(pair * 2 + (LOOP_FROM + 1))
            for i in range(LOOP_TO, B + 2):
                iteration(i)

        n_weights = 16 * (5 + 2 * DC + 2)
        LAST_IN_BANK = [max(c for c in range(CROSS_CHUNKS) if c % NSCORE == j) for j in range(NSCORE)]
        assert SELF_CHUNKS % NSCORE == 0
        block = es.enter_context(nc.Block())

        @block.sync
        def _(sp):
            def rows(i, lag):
                if isinstance(i, int):
                    return slice((i - lag) * T, (i - lag + 1) * T)
                return bass.ds(plus(i, T, -lag * T), T)

            def tokens(ap, i, lag):
                return ap[rows(i, lag), :].rearrange("(t p) d -> p t d", p=P)

            def load(i, lag, dst, src, name):
                sp.dma_start(dst[:, :, :], tokens(src, i, lag)).then_inc(signal[name], 16)

            sp.dma_start(x_in[:, :, :], tokens(x, 0, 0)).then_inc(signal["x_in"], 16)
            sp.dma_start(wa[:, :, :], w_attn.rearrange("(c p) n -> p c n", p=P)).then_inc(wa_in, 16)
            for dst, src in ((wqx, wq), (wkvx, wkv), (wp, w_proj), (wpx, wproj), (wf_raw, ffn_w)):
                sp.dma_start(dst[:, :, :], src.rearrange("(c p) n -> p c n", p=P)).then_inc(weights_in, 16)
            for dst, src in ((qg, q_gamma), (kg, k_gamma)):
                for c in range(DC):
                    sp.dma_start(dst[:, c:c + 1], src[c * HC:(c + 1) * HC].unsqueeze(1).to_broadcast([HC, H]))\
                        .then_inc(weights_in, 16)
            for dst, src in ((fscale, ffn_scale), (fbias, ffn_bias)):
                sp.dma_start(dst[:, :], src.partition_broadcast(P)).then_inc(weights_in, 16)

            def load_x(i, k, lag):
                if not (isinstance(i, int) and i - lag == 0):
                    last = use(i, "xT", 0, back=1)
                    if last:
                        sp.wait_ge(last.filled, last.n + 1)
                        sp.sem_inc(passed_sp, 1)
                    load(i, lag, x_in, x, "x_in")

            def load_ctx(i, k, lag):
                last = use(i, "cT", 0, back=1)
                if last:
                    sp.wait_ge(last.filled, last.n + 1)
                    sp.sem_inc(passed_sp, 1)
                load(i, lag, ctx, ctx_in_d, "ctx_in")

            def load_res(i, k, lag):
                source = use(i, "t3S", 0, back=1)
                if source:
                    sp.wait_ge(source.drained, source.n + 1)
                    sp.sem_inc(passed_sp, 1)
                load(i, lag, x_res, x, "x_res")

            def spilling(tag, parts):
                def emit(i, k, lag):
                    sp.wait_ge(signal[tag + "_low"], count(i, lag, tag + "_low"))
                    sp.sem_inc(passed_sp, 1)
                    if some(i, lag + 1):
                        sp.wait_ge(signal[tag + "_stacked"], count(i, lag + 1, tag + "_stacked"))
                        sp.sem_inc(passed_sp, 1)
                    sp.dma_start(spill[tag].rearrange("a c p t -> p (a c) t"),
                                 parts[:, :, :, :].rearrange("p a c t -> p (a c) t"))\
                        .then_inc(signal[tag + "_spilled"], 16)
                return emit

            def stacking(tag, runs, dst, scores):
                def emit(i, k, lag):
                    if some(i, lag + 1):
                        sp.wait_ge(signal[scores], count(i, lag + 1, scores))
                        sp.sem_inc(passed_sp, 1)
                    sp.wait_ge(signal[tag + "_spilled"], count(i, lag, tag + "_spilled"))
                    sp.sem_inc(passed_sp, 1)
                    src = spill[tag].rearrange("a c (e h) t -> (a c e) h t", h=H)
                    for slot, part, n in runs:
                        sp.dma_start(dst[slot * HD:(slot + n) * HD, :, :], src[part * HD:(part + n) * HD, :, :])\
                            .then_inc(signal[tag + "_stacked"], 16)
                return emit

            def max_rows(i, lag, tag, neg, dst):
                source = use(i, "m" + tag, 0)
                sp.wait_ge(source.drained, source.n + 1)
                sp.sem_inc(passed_sp, 1)
                for part in range(2):
                    sp.dma_start(dst[QK_ROWS + part:QK_ROWS + part + 1, :, :], neg[:, part, :])\
                        .then_inc(signal[f"max{tag}_stacked"], 16)

            def mS(i, k, lag):
                if some(i, lag + 1):
                    sp.wait_ge(signal["scoresS"], count(i, lag + 1, "scoresS"))
                    sp.sem_inc(passed_sp, 1)
                max_rows(i, lag, "S", negS, qaS)

            def mX(i, k, lag):
                if some(i, lag + 1):
                    sp.wait_ge(signal["scoresX"], count(i, lag + 1, "scoresX"))
                    sp.sem_inc(passed_sp, 1)
                max_rows(i, lag, "X", negX, qaX)

            def ln3(i, k, lag):
                sp.wait_ge(signal["x3"], count(i, lag, "x3"))
                sp.sem_inc(passed_sp, 1)
                sp.dma_start(tokens(out, i, lag), x3[:, :, :]).then_inc(signal["stored"], 16)

            run(sp, {"load_x": load_x, "load_ctx": load_ctx, "load_res": load_res, "qLow": spilling("qS", partS),
                     "qS3": stacking("qS", Q_RUNS, qaS, "scoresS"), "kXLow": spilling("kX", partX["k"]),
                     "kX3": stacking("kX", K_RUNS, kaX, "scoresX"),
                     "qXLow": spilling("qX", partX["q"]), "qX3": stacking("qX", Q_RUNS, qaX, "scoresX"), "mS": mS,
                     "mX": mX, "ln3": ln3})
            sp.wait_ge(signal["stored"], 16 * B)

        @block.tensor
        def _(pe):
            def transpose_tokens(i, step, src):
                w = use(i, step, 0)
                if w.used:
                    pe.wait_ge(w.drained, w.n)
                for c in range(DC):
                    for t in range(TT):
                        mm = pe.transpose(w[:, c * T + t * P:c * T + (t + 1) * P], src[:, t, c * P:(c + 1) * P],
                                          ident[:, :])
                mm.then_inc(w.filled, 1)

            def project_tokens(i, step, k, srcT, weights, tile_at):
                w = use(i, step, k)
                if w.used:
                    pe.wait_ge(w.drained, w.n)
                n = weights.shape[2]
                for t, col in tile_at.items():
                    for c in range(DC):
                        mm = pe.matmul(w[:, col:col + n], srcT[:, c, t * P:(t + 1) * P], weights[:, c, :],
                                       start=(c == 0), stop=(c == DC - 1))
                mm.then_inc(w.filled, 1)

            def xT_(i, k, lag):
                pe.wait_ge(signal["x_in"], count(i, lag, "x_in"))
                transpose_tokens(i, "xT", x_in)

            def qS(i, k, lag):
                source = use(i, "xT", 0)
                pe.wait_ge(source.drained, source.n + 1)
                w = use(i, "qS", 0)
                if w.used:
                    pe.wait_ge(w.drained, w.n)
                for m in range(DC):
                    for c in range(DC):
                        mm = pe.matmul(w[:, m * T:(m + 1) * T], waq[:, c, m * P:(m + 1) * P], xT[:, c, :],
                                       start=(c == 0), stop=(c == DC - 1))
                mm.then_inc(w.filled, 1)

            def kvS(i, k, lag):
                source = use(i, "xT", 0)
                pe.wait_ge(source.drained, source.n + 1)
                project_tokens(i, "kvS", 0, xT, wa[:, :, D:D + 2 * HD], {0: 0, 1: 2 * HD})

            def kS(i, k, lag):
                pe.wait_ge(signal["k_tok"], count(i, lag, "k_tok"))
                w = use(i, "kS", 0)
                if w.used:
                    pe.wait_ge(w.drained, w.n)
                for t in range(TT):
                    mm = pe.matmul(w[0:QK_ROWS, t * P:(t + 1) * P], ktok[:, t, :, :].rearrange("p s d -> p (s d)"),
                                   ident[:, :], start=True, stop=True)
                mm.then_inc(w.filled, 1)

            def maxS_(i, u, lag):
                if u == 0:
                    pe.wait_ge(signal["qS_stacked"], count(i, lag, "qS_stacked"))
                    pe.wait_ge(signal["kS_low"], count(i, lag, "kS_low"))
                w = use(i, "maxS", u)
                if w.used:
                    pe.wait_ge(w.drained, w.n)
                if u < 8:
                    for j in range(2):
                        pe.matmul(w[:, j * T:(j + 1) * T], qaS[0:QK_ROWS, 2 * u + j, P:T], kaS[0:QK_ROWS, :],
                                  start=(j == 0), stop=False, skip_group_check=True)
                    mm = pe.matmul(w[:, :].rearrange("p (h k) -> p h k", h=2)[:, :, P:T], identb[:, :],
                                   causal[:, 0:2, :], start=False, stop=True, skip_group_check=True)
                else:
                    for j in range(4):
                        pe.matmul(w[:, j * P:(j + 1) * P], qaS[0:QK_ROWS, 4 * (u - 8) + j, 0:P], kaS[0:QK_ROWS, 0:P],
                                  start=(j == 0), stop=False, skip_group_check=True)
                    mm = pe.matmul(w[:, :], identb[:, :], causal[:, :, :].rearrange("p h k -> p (h k)"),
                                   start=False, stop=True, skip_group_check=True)
                mm.then_inc(w.filled, 1)

            def maxX_(i, u, lag):
                if u == 0:
                    pe.wait_ge(signal["qX_stacked"], count(i, lag, "qX_stacked"))
                    pe.wait_ge(signal["kX_stacked"], count(i, lag, "kX_stacked"))
                w = use(i, "maxX", u)
                if w.used:
                    pe.wait_ge(w.drained, w.n)
                t, h = u // 8, 2 * (u % 8)
                for j in range(2):
                    mm = pe.matmul(w[:, j * T:(j + 1) * T], qaX[0:QK_ROWS, h + j, t * P:(t + 1) * P],
                                   kaX[0:QK_ROWS, h + j, :], start=True, stop=True)
                mm.then_inc(w.filled, 1)

            def turn_max(i, step, last, src):
                source = use(i, *last)
                pe.wait_ge(source.drained, source.n + 1)
                w = use(i, step, 0)
                if w.used:
                    pe.wait_ge(w.drained, w.n)
                for t in range(TT):
                    mm = pe.matmul(w[0:H, t * P:(t + 1) * P], src[:, t, :], ident[:, :], start=True, stop=True)
                mm.then_inc(w.filled, 1)

            def qkS(i, c, lag):
                if c == 0:
                    pe.wait_ge(signal["maxS_stacked"], count(i, lag, "maxS_stacked"))
                if c >= NSCORE:
                    pe.wait_ge(signal["expS"], count(i, lag, "expS", c - NSCORE + 1))
                elif some(i, lag + 2):
                    pe.wait_ge(signal["expX"], count(i, lag + 2, "expX", LAST_IN_BANK[c] + 1))
                s = score[c % NSCORE]
                n, j = c // 2, c % 2
                if n % 3 < 2:
                    h = 8 * (n // 3) + 4 * (n % 3) + 2 * j
                    pe.matmul(s[:, :], kaS[:, 0:P], qaS[:, h:h + 2, :], start=True, stop=True)\
                        .then_inc(signal["scoresS"], 1)
                else:
                    h = 8 * (n // 3) + 4 * j
                    pe.matmul(s[:, :], kaS[:, P:T], qaS[:, h:h + 4, P:T], start=True, stop=True)\
                        .then_inc(signal["scoresS"], 1)

            def qkX(i, c, lag):
                if c == 0:
                    pe.wait_ge(signal["maxX_stacked"], count(i, lag, "maxX_stacked"))
                if c >= NSCORE:
                    pe.wait_ge(signal["expX"], count(i, lag, "expX", c - NSCORE + 1))
                elif some(i, lag - 1):
                    pe.wait_ge(signal["expS"], count(i, lag - 1, "expS", SELF_CHUNKS - NSCORE + c + 1))
                s = score[c % NSCORE]
                kt, h = c // 2 % 2, 4 * (c // 4) + 2 * (c % 2)
                for j in range(2):
                    mm = pe.matmul(s[:, j * T:(j + 1) * T], kaX[:, h + j, kt * P:(kt + 1) * P], qaX[:, h + j, :],
                                   start=True, stop=True)
                mm.then_inc(signal["scoresX"], 1)

            def pvS(i, n, lag):
                half = n // 3
                pe.wait_ge(signal["maskedS"], count(i, lag, "maskedS", n + 1))
                if n == 0:
                    pe.wait_ge(signal["vS_placed"], count(i, lag, "vS_placed"))
                    if some(i, lag + 2):
                        pe.wait_ge(signal["otX"], count(i, lag + 2, "otX"))
                if n == 3:
                    pe.wait_ge(signal["otS"], count(i, lag, "otS", 1))
                if n % 3 < 2:
                    g = 2 * half + n % 3
                    for j in range(4):
                        pe.matmul(out_bank[32 * j:32 * (j + 1), (n % 3) * T:(n % 3 + 1) * T], vaS[:, 0, :],
                                  ptS0[:, 4 * g + j, :], start=(n % 3 == 0), stop=False, skip_group_check=True)
                else:
                    for gg in range(2):
                        for j in range(4):
                            mm = pe.matmul(out_bank[32 * j:32 * (j + 1), gg * T + P:(gg + 1) * T], vaS[:, 1, :],
                                           ptS1[:, 8 * half + 4 * gg + j, :], start=False, stop=True,
                                           skip_group_check=True)
                    mm.then_inc(signal["pvS"], 1)

            def pvX(i, n, lag):
                g, kt = n // 2, n % 2
                pe.wait_ge(signal["expX"], count(i, lag, "expX", 2 * n + 2))
                if n == 0:
                    pe.wait_ge(signal["v_placed"], count(i, lag, "v_placed"))
                    if some(i, lag - 1):
                        pe.wait_ge(signal["otS"], count(i, lag - 1, "otS"))
                if n == 4:
                    pe.wait_ge(signal["otX"], count(i, lag, "otX", 1))
                for j in range(4):
                    h = 4 * g + j
                    mm = pe.matmul(out_bank[32 * j:32 * (j + 1), (g % 2) * T:(g % 2 + 1) * T], vaX[:, kt, h, :],
                                   ptX[:, kt, h, :], start=(kt == 0), stop=(kt == 1), skip_group_check=True)
                if n % 4 == 3:
                    mm.then_inc(signal["pvX"], 1)

            def t1(tag):
                def step(i, t, lag):
                    pe.wait_ge(signal["ot" + tag], count(i, lag, "ot" + tag))
                    w = use(i, "t1" + tag, t)
                    if w.used:
                        pe.wait_ge(w.drained, w.n)
                    for g in range(4):
                        mm = pe.transpose(w[:, g * P:(g + 1) * P], ot[tag][:, g, t * P:(t + 1) * P], ident[:, :])
                    mm.then_inc(w.filled, 1)
                return step

            def t2(tag):
                def step(i, k, lag):
                    source = use(i, "t1" + tag, 1)
                    pe.wait_ge(source.drained, source.n + 1)
                    transpose_tokens(i, "t2" + tag, on[tag])
                return step

            def t3(tag, weights):
                def step(i, k, lag):
                    source = use(i, "t2" + tag, 0)
                    pe.wait_ge(source.drained, source.n + 1)
                    project_tokens(i, "t3" + tag, 0, onT[tag], weights, {0: 0, 1: D})
                return step

            def cT(i, k, lag):
                pe.wait_ge(signal["ctx_in"], count(i, lag, "ctx_in"))
                transpose_tokens(i, "cT", ctx)

            def kv(i, t, lag):
                source = use(i, "cT", 0)
                pe.wait_ge(source.drained, source.n + 1)
                project_tokens(i, "kv", t, ctxT, wkvx, {t: 0})

            def kX(i, k, lag):
                pe.wait_ge(signal["k_norm"], count(i, lag, "k_norm"))
                transpose_tokens(i, "kX", normed["k"])

            def x1T_(i, k, lag):
                pe.wait_ge(signal["x1"], count(i, lag, "x1"))
                transpose_tokens(i, "x1T", x1)

            def q_(i, k, lag):
                source = use(i, "x1T", 0)
                pe.wait_ge(source.drained, source.n + 1)
                project_tokens(i, "q", 0, x1T, wqx, {0: 0, 1: D})

            def qX(i, k, lag):
                pe.wait_ge(signal["q_norm"], count(i, lag, "q_norm"))
                transpose_tokens(i, "qX", normed["q"])

            def x2T_(i, k, lag):
                pe.wait_ge(signal["x2"], count(i, lag, "x2"))
                transpose_tokens(i, "x2T", x2)

            def ffn(i, k, lag):
                source = use(i, "x2T", 0)
                pe.wait_ge(source.drained, source.n + 1)
                project_tokens(i, "ffn", 0, x2T, wfT, {0: 0, 1: D})

            def set_up():
                pe.wait_ge(ones_set, 5)
                pe.wait_ge(weights_in, n_weights)
                pe.wait_ge(sign_set, 2)
                w = use(0, "wT", 0)
                pe.wait_ge(w.drained, w.n)
                for c in range(DC):
                    for o in range(DC):
                        mm = pe.transpose(w[:, c * D + o * P:c * D + (o + 1) * P], wf_sign[:, o, c * P:(c + 1) * P],
                                          ident[:, :])
                mm.then_inc(w.filled, 1)

            pe.wait_ge(const_set, 5)
            pe.wait_ge(waq_set, DC)
            run(pe, {"xT": xT_, "qS": qS, "kvS": kvS, "kS": kS, "maxS": maxS_, "maxX": maxX_,
                     "mS": lambda i, k, lag: turn_max(i, "mS", ("maxS", MAX_S - 1), maxS),
                     "mX": lambda i, k, lag: turn_max(i, "mX", ("maxX", MAX_X - 1), maxX),
                     "qkS": qkS, "qkX": qkX, "pvS": pvS, "pvX": pvX, "t1S": t1("S"), "t1X": t1("X"),
                     "t2S": t2("S"), "t2X": t2("X"), "t3S": t3("S", wp), "t3X": t3("X", wpx), "cT": cT, "kv": kv,
                     "kX": kX, "x1T": x1T_, "q": q_, "qX": qX, "x2T": x2T_, "ffn": ffn}, set_up)

        @block.scalar
        def _(act):
            def flat(tile):
                return tile[:, :, :].rearrange("p c t -> p (c t)")

            def copy_out(step, dst, product, product_k=0):
                def emit(i, k, lag):
                    last = use(i, product, product_k, back=1)
                    if last:
                        act.wait_ge(last.filled, last.n + 1)
                    w = use(i, step, 0)
                    act.wait_ge(w.filled, w.n + 1)
                    act.activation(flat(dst), w[:, :], ACT.Copy).then_inc(w.drained, 1)
                return emit

            def kv(i, t, lag):
                if some(i, lag + 1):
                    act.wait_ge(signal["k_norm"], count(i, lag + 1, "k_norm"))
                    act.wait_ge(signal["v_placed"], count(i, lag + 1, "v_placed"))
                w = use(i, "kv", t)
                act.wait_ge(w.filled, w.n + 1)
                act.activation(kvraw[:, t, :], w[:, :], ACT.Copy).then_inc(w.drained, 1)

            def q_(i, k, lag):
                if some(i, lag + 1):
                    act.wait_ge(signal["q_norm"], count(i, lag + 1, "q_norm"))
                w = use(i, "q", 0)
                act.wait_ge(w.filled, w.n + 1)
                act.activation(flat(qraw), w[:, :], ACT.Copy).then_inc(w.drained, 1)

            def qS(i, k, lag):
                w = use(i, "qS", 0)
                act.wait_ge(w.filled, w.n + 1)
                if some(i, lag + 1):
                    act.wait_ge(signal["qS_spilled"], count(i, lag + 1, "qS_spilled"))
                act.activation(partS[:, 0, :, :], w[:, :].rearrange("p (c t) -> p c t", c=DC), ACT.Copy)\
                    .then_inc(signal["qS_high"], 1)

            def kS(i, k, lag):
                w = use(i, "kS", 0)
                act.wait_ge(w.filled, w.n + 1)
                last = use(i, "kS", 0, back=1)
                if last:
                    act.wait_ge(last.drained, last.n + 1)
                act.activation(highK[:, :], w[0:QK_ROWS, 0:T], ACT.Copy).then_inc(signal["kS_high"], 1)

            def kvS(i, k, lag):
                last = use(i, "kS", 0, back=1)
                if last:
                    act.wait_ge(last.filled, last.n + 1)
                w = use(i, "kvS", 0)
                act.wait_ge(w.filled, w.n + 1)
                kv = w[:, 0:TT * 2 * HD].rearrange("p (t e) -> p t e", t=TT)
                act.activation(ktok[:, :, :, :], kv[:, :, 0:HD].unsqueeze(2).to_broadcast([P, TT, SLOTS, HD]), ACT.Copy)\
                    .then_inc(signal["k_tok"], 1)
                act.activation(vtok[:, :, :], kv[:, :, HD:2 * HD], ACT.Copy).then_inc(w.drained, 1)

            def vS(i, k, lag):
                if some(i, lag + 1):
                    act.wait_ge(signal["pvS"], count(i, lag + 1, "pvS"))
                source = use(i, "kvS", 0)
                act.wait_ge(source.drained, source.n + 1)
                act.wait_ge(ones_set, 3)
                act.activation(vaS[:, :, 0:HD], vtok[:, :, :], ACT.Copy).then_inc(signal["vS_placed"], 1)

            def qMid(i, k, lag):
                source = use(i, "qS", 0)
                act.wait_ge(source.drained, source.n + 1)
                act.activation(partS[:, 1, :, :], restS[:, :, :], ACT.Copy).then_inc(signal["qS_mid"], 1)
                source = use(i, "kS", 0)
                act.wait_ge(source.drained, source.n + 1)
                if some(i, lag + 1):
                    act.wait_ge(signal["kS_low"], count(i, lag + 1, "kS_low"))
                act.activation(midK[:, :], restK[:, :], ACT.Copy).then_inc(signal["kS_mid"], 1)

            def neg_high(tag, neg):
                def emit(i, k, lag):
                    w = use(i, "m" + tag, 0)
                    act.wait_ge(w.filled, w.n + 1)
                    if some(i, lag + 1):
                        act.wait_ge(signal[f"max{tag}_stacked"], count(i, lag + 1, f"max{tag}_stacked"))
                    act.activation(neg[:, 0, :], w[0:H, 0:T], ACT.Copy, scale=-1.0)\
                        .then_inc(signal[f"max{tag}_high"], 1)
                return emit

            def expS(i, c, lag):
                act.wait_ge(signal["scoresS"], count(i, lag, "scoresS", c + 1))
                n, j = c // 2, c % 2
                if some(i, lag + 1):
                    act.wait_ge(signal["pvS"], count(i, lag + 1, "pvS", n // 3 + 1))
                if n % 3 < 2:
                    h = 8 * (n // 3) + 4 * (n % 3) + 2 * j
                    dst = ptS0[:, h:h + 2, :]
                else:
                    h = 8 * (n // 3) + 4 * j
                    dst = ptS1[:, h:h + 4, :]
                act.activation(dst.rearrange("p h q -> p (h q)"), score[c % NSCORE][:, :], ACT.Exp, scale=SCALE)\
                    .then_inc(signal["expS"], 1)

            def expX(i, c, lag):
                act.wait_ge(signal["scoresX"], count(i, lag, "scoresX", c + 1))
                if some(i, lag + 1):
                    act.wait_ge(signal["pvX"], count(i, lag + 1, "pvX", c // 8 + 1))
                kt, h = c // 2 % 2, 4 * (c // 4) + 2 * (c % 2)
                act.activation(ptX[:, kt, h:h + 2, :].rearrange("p h q -> p (h q)"), score[c % NSCORE][:, :],
                               ACT.Exp, scale=SCALE).then_inc(signal["expX"], 1)

            def otev(tag):
                def emit(i, half, lag):
                    act.wait_ge(signal["pv" + tag], count(i, lag, "pv" + tag, half + 1))
                    last = use(i, "t1" + tag, 1, back=1)
                    if last:
                        act.wait_ge(last.filled, last.n + 1)
                    act.activation(ot[tag][:, 2 * half:2 * half + 2, :].rearrange("p g t -> p (g t)"), out_bank[:, :],
                                   ACT.Copy).then_inc(signal["ot" + tag], 1)
                return emit

            def square(n, src, step, last_k):
                def emit(i, k, lag):
                    source = use(i, step, last_k)
                    act.wait_ge(source.drained, source.n + 1)
                    if some(i, lag + 1):
                        act.wait_ge(signal[n + "_ss"], count(i, lag + 1, n + "_ss"))
                    act.activation(squares[n][:, :, :], src, ACT.Square).then_inc(signal[n + "_sq"], 1)
                return emit

            def kX(i, k, lag):
                w = use(i, "kX", 0)
                act.wait_ge(w.filled, w.n + 1)
                if some(i, lag + 1):
                    act.wait_ge(signal["kX_spilled"], count(i, lag + 1, "kX_spilled"))
                act.wait_ge(gamma_set, 1)
                for c in range(DC):
                    act.activation(partX["k"][:, 0, c, :], w[:, c * T:(c + 1) * T], ACT.Copy, scale=gamma[:, c:c + 1])\
                        .then_inc(signal["kX_high"], 1)

            def qX(i, k, lag):
                w = use(i, "qX", 0)
                act.wait_ge(w.filled, w.n + 1)
                if some(i, lag + 1):
                    act.wait_ge(signal["qX_spilled"], count(i, lag + 1, "qX_spilled"))
                act.activation(partX["q"][:, 0, :, :], w[:, :].rearrange("p (c t) -> p c t", c=DC), ACT.Copy)\
                    .then_inc(signal["qX_high"], 1)

            def mid(n):
                def emit(i, k, lag):
                    if n == "k":
                        act.wait_ge(signal["kX_rest"], count(i, lag, "kX_rest"))
                    source = use(i, n + "X", 0)
                    act.wait_ge(source.drained, source.n + 1)
                    act.activation(partX[n][:, 1, :, :], restX[n][:, :, :], ACT.Copy).then_inc(signal[n + "X_mid"], 1)
                return emit


            run(act, {
                "xT": copy_out("xT", xT, "qS"), "qS": qS, "kvS": kvS, "kS": kS, "vS": vS, "qMid": qMid,
                "cT": copy_out("cT", ctxT, "kv", 1), "kv": kv, "kSq": square("k", kvraw[:, :, 0:D], "kv", 1),
                "kX": kX, "kXMid": mid("k"), "qX": qX, "qXMid": mid("q"),
                "x1T": copy_out("x1T", x1T, "q"), "q": q_, "qSq": square("q", qraw[:, :, :], "q", 0),
                "x2T": copy_out("x2T", x2T, "ffn"),
                "t2S": copy_out("t2S", onT["S"], "t3S"), "t2X": copy_out("t2X", onT["X"], "t3X"),
                "mS": neg_high("S", negS), "mX": neg_high("X", negX),
                "qkS": expS, "qkX": expX, "otS": otev("S"), "otX": otev("X"),
            })

        @block.vector
        def _(dve):
            dve.memset(halfpow[:, :], -0.5).then_inc(ones_set, 1)
            dve.memset(kaS[QK_ROWS:ROWS, :], 1.0).then_inc(ones_set, 1)
            dve.memset(vaS[:, :, :], 1.0).then_inc(ones_set, 1)
            dve.wait_ge(wa_in, 16)
            for c in range(DC):
                dve.tensor_copy(waq[:, c, :].rearrange("p (d h) -> p h d", d=HD),
                                wa[:, c, 0:D].rearrange("p (h d) -> p h d", d=HD)).then_inc(waq_set, 1)
            dve.wait_ge(const_set, 8)

            def set_up():
                dve.memset(kaX[QK_ROWS:ROWS, :, :].rearrange("p h t -> p (h t)"), 1.0).then_inc(ones_set, 1)
                dve.memset(vaX[:, :, :, :].rearrange("p t h d -> p (t h d)"), 1.0).then_inc(ones_set, 1)
                dve.wait_ge(weights_in, n_weights)
                dve.tensor_tensor(gamma[:, :], qg[:, :], kg[:, :], ALU.mult).then_inc(gamma_set, 1)
                dve.tensor_scalar(wf_ge[:, :, :], wf_raw[:, :, :], 0.0, 2.0, ALU.is_ge, ALU.mult).then_inc(sign_set, 1)
                dve.wait_ge(sign_set, 1)
                dve.tensor_scalar(wf_sign[:, :, :], wf_ge[:, :, :], -1.0, None, ALU.add).then_inc(sign_set, 1)
                w = use(0, "wT", 0)
                dve.wait_ge(w.filled, w.n + 1)
                dve.tensor_tensor(wfT[:, :, :], w[:, :].rearrange("p (c o) -> p c o", c=DC),
                                  fscale[:, :].unsqueeze(1).to_broadcast([P, DC, D]), ALU.mult).then_inc(w.drained, 1)

            def qRest(i, k, lag):
                w = use(i, "qS", 0)
                dve.wait_ge(w.filled, w.n + 1)
                dve.wait_ge(signal["qS_high"], count(i, lag, "qS_high"))
                if some(i, lag + 1):
                    dve.wait_ge(signal["qS_low"], count(i, lag + 1, "qS_low"))
                dve.tensor_tensor(restS[:, :, :], w[:, :].rearrange("p (c t) -> p c t", c=DC), partS[:, 0, :, :],
                                  ALU.subtract).then_inc(w.drained, 1)
                w = use(i, "kS", 0)
                dve.wait_ge(w.filled, w.n + 1)
                dve.wait_ge(signal["kS_high"], count(i, lag, "kS_high"))
                if some(i, lag + 1):
                    dve.wait_ge(signal["kS_low"], count(i, lag + 1, "kS_low"))
                dve.scalar_tensor_tensor(restK[:, :], highK[:, :], kdrop[:, 0:1], w[0:QK_ROWS, 0:T], ALU.mult, ALU.add)\
                    .then_inc(w.drained, 1)

            def qLow(i, k, lag):
                dve.wait_ge(signal["qS_mid"], count(i, lag, "qS_mid"))
                dve.tensor_tensor(partS[:, 2, :, :], restS[:, :, :], partS[:, 1, :, :], ALU.subtract)\
                    .then_inc(signal["qS_low"], 1)

            def kLow(i, k, lag):
                dve.wait_ge(signal["kS_mid"], count(i, lag, "kS_mid"))
                if some(i, lag + 1):
                    dve.wait_ge(signal["scoresS"], count(i, lag + 1, "scoresS"))
                dve.scalar_tensor_tensor(kaS[0:QK_ROWS, :], midK[:, :], kdrop[:, 1:2], restK[:, :], ALU.mult, ALU.add)\
                    .then_inc(signal["kS_low"], 1)

            def maxS_(i, u, lag):
                if u == 0:
                    last = use(i, "mS", 0, back=1)
                    if last:
                        dve.wait_ge(last.filled, last.n + 1)
                w = use(i, "maxS", u)
                dve.wait_ge(w.filled, w.n + 1)
                if u < 8:
                    dve.tensor_reduce(maxS[:, 1, 2 * u:2 * u + 2], w[:, :].rearrange("p (h k) -> p h k", h=2), AX.X,
                                      ALU.max).then_inc(w.drained, 1)
                else:
                    dve.tensor_reduce(maxS[:, 0, 4 * (u - 8):4 * (u - 8) + 4], w[:, :].rearrange("p (h k) -> p h k", h=4),
                                      AX.X, ALU.max).then_inc(w.drained, 1)

            def maxX_(i, u, lag):
                if u == 0:
                    last = use(i, "mX", 0, back=1)
                    if last:
                        dve.wait_ge(last.filled, last.n + 1)
                w = use(i, "maxX", u)
                dve.wait_ge(w.filled, w.n + 1)
                t, h = u // 8, 2 * (u % 8)
                dve.tensor_reduce(maxX[:, t, h:h + 2], w[:, :].rearrange("p (h k) -> p h k", h=2), AX.X, ALU.max)\
                    .then_inc(w.drained, 1)

            def neg_low(tag, neg):
                def emit(i, k, lag):
                    w = use(i, "m" + tag, 0)
                    dve.wait_ge(w.filled, w.n + 1)
                    dve.wait_ge(signal[f"max{tag}_high"], count(i, lag, f"max{tag}_high"))
                    if some(i, lag + 1):
                        dve.wait_ge(signal[f"max{tag}_stacked"], count(i, lag + 1, f"max{tag}_stacked"))
                    dve.scalar_tensor_tensor(neg[:, 1, :], w[0:H, 0:T], -1.0, neg[:, 0, :], ALU.mult, ALU.subtract)\
                        .then_inc(w.drained, 1)
                return emit

            def normalise(tag):
                def emit(i, t, lag):
                    w = use(i, "t1" + tag, t)
                    dve.wait_ge(w.filled, w.n + 1)
                    last = use(i, "t2" + tag, 0, back=1)
                    if last:
                        dve.wait_ge(last.filled, last.n + 1)
                    o = w[:, :].rearrange("p (h e) -> p h e", e=2 * HD)
                    dve.reciprocal(rden[tag][:, t, :], o[:, :, HD]).then_inc(signal["rden" + tag], 1)
                    dve.wait_ge(signal["rden" + tag], count(i, lag, "rden" + tag, t + 1))
                    dve.tensor_tensor(on[tag][:, t, :].rearrange("p (h d) -> p h d", d=HD), o[:, :, 0:HD],
                                      rden[tag][:, t, :].unsqueeze(2).to_broadcast([P, H, HD]), ALU.mult)\
                        .then_inc(w.drained, 1)
                return emit

            def moments(n, src, summed):
                def stat(i, k, lag):
                    summed(i, lag)
                    for t in range(TT):
                        dve.bn_stats(stats[n][:, t, :], src[:, t, :]).then_inc(signal[f"ln{n}_stats"], 1)

                def aggr(i, k, lag):
                    for t in range(TT):
                        dve.wait_ge(signal[f"ln{n}_stats"], count(i, lag, f"ln{n}_stats", t + 1))
                        dve.sem_inc(passed_dve, 1)
                        dve.bn_aggr(mv[n][:, t, :], stats[n][:, t, :]).then_inc(signal[f"ln{n}_aggr"], 1)
                return stat, aggr

            def residual(tag, n, total, res, res_ready):
                def emit(i, k, lag):
                    w = use(i, "t3" + tag, 0)
                    dve.wait_ge(w.filled, w.n + 1)
                    dve.wait_ge(signal[res_ready], count(i, lag, res_ready))
                    if some(i, lag + 1):
                        dve.wait_ge(signal[f"x{n}"], count(i, lag + 1, f"x{n}"))
                    dve.tensor_tensor(total[:, :, :].rearrange("p t d -> p (t d)"), w[:, :],
                                      res[:, :, :].rearrange("p t d -> p (t d)"), ALU.add).then_inc(w.drained, 1)
                return emit

            def sum1_there(i, lag):
                w = use(i, "t3S", 0)
                dve.wait_ge(w.drained, w.n + 1)

            def sum2_there(i, lag):
                w = use(i, "t3X", 0)
                dve.wait_ge(w.drained, w.n + 1)

            def sum3_there(i, lag):
                dve.wait_ge(signal["f_sum"], count(i, lag, "f_sum"))

            stats1, aggr1 = moments(1, sum1, sum1_there)
            stats2, aggr2 = moments(2, sum2, sum2_there)
            stats3, aggr3 = moments(3, sum3, sum3_there)

            def apply_norm(i, lag, n, src, dst):
                dve.wait_ge(signal[f"ln{n}_rstd"], count(i, lag, f"ln{n}_rstd"))
                for t in range(TT):
                    dve.tensor_scalar(dst[:, t, :], src[:, t, :], mv[n][:, t, 0:1], rstd[n][:, t:t + 1],
                                      ALU.subtract, ALU.mult).then_inc(signal[f"x{n}"], 1)

            def ln1(i, k, lag):
                if some(i, lag + 1):
                    dve.wait_ge(signal["x1_kept"], count(i, lag + 1, "x1_kept"))
                last = use(i, "x1T", 0, back=1)
                if last:
                    dve.wait_ge(last.filled, last.n + 1)
                apply_norm(i, lag, 1, sum1, x1)

            def ln2(i, k, lag):
                if some(i, lag + 1):
                    dve.wait_ge(signal["f_sum"], count(i, lag + 1, "f_sum"))
                apply_norm(i, lag, 2, sum2, x2)

            def ln3(i, k, lag):
                if some(i, lag + 1):
                    dve.wait_ge(signal["stored"], count(i, lag + 1, "stored"))
                apply_norm(i, lag, 3, sum3, x3)

            def sum_squares(n):
                def emit(i, k, lag):
                    dve.wait_ge(signal[n + "_sq"], count(i, lag, n + "_sq"))
                    if some(i, lag + 1):
                        dve.wait_ge(signal[n + "_ms"], count(i, lag + 1, n + "_ms"))
                    dve.tensor_reduce(ss[n][:, :], squares[n][:, :, :].rearrange("p t (h d) -> p (t h) d", d=HD), AX.X,
                                      ALU.add).then_inc(signal[n + "_ss"], 1)
                return emit

            def rms(n, src, step):
                def emit(i, k, lag):
                    dve.wait_ge(signal[n + "_rs"], count(i, lag, n + "_rs"))
                    last = use(i, step, 0, back=1)
                    if last:
                        dve.wait_ge(last.filled, last.n + 1)
                    dve.tensor_tensor(normed[n][:, :, :].rearrange("p t (d h) -> p t h d", d=HD),
                                      src.rearrange("p t (h d) -> p t h d", d=HD),
                                      rs[n][:, :].rearrange("p (t h) -> p t h", t=TT).unsqueeze(3)
                                      .to_broadcast([P, TT, H, HD]), ALU.mult).then_inc(signal[n + "_norm"], 1)
                return emit

            def kXRest(i, k, lag):
                w = use(i, "kX", 0)
                dve.wait_ge(w.filled, w.n + 1)
                dve.wait_ge(signal["kX_high"], count(i, lag, "kX_high"))
                if some(i, lag + 1):
                    dve.wait_ge(signal["kX_low"], count(i, lag + 1, "kX_low"))
                for c in range(DC):
                    done = signal["kX_rest"] if c < DC - 1 else w.drained
                    dve.scalar_tensor_tensor(restX["k"][:, c, :], w[:, c * T:(c + 1) * T], gamma[:, c:c + 1],
                                             partX["k"][:, 0, c, :], ALU.mult, ALU.subtract).then_inc(done, 1)

            def qXRest(i, k, lag):
                w = use(i, "qX", 0)
                dve.wait_ge(w.filled, w.n + 1)
                dve.wait_ge(signal["qX_high"], count(i, lag, "qX_high"))
                if some(i, lag + 1):
                    dve.wait_ge(signal["qX_low"], count(i, lag + 1, "qX_low"))
                dve.tensor_tensor(restX["q"][:, :, :], w[:, :].rearrange("p (c t) -> p c t", c=DC),
                                  partX["q"][:, 0, :, :], ALU.subtract).then_inc(w.drained, 1)

            def low(n):
                def emit(i, k, lag):
                    dve.wait_ge(signal[n + "X_mid"], count(i, lag, n + "X_mid"))
                    dve.tensor_tensor(partX[n][:, 2, :, :], restX[n][:, :, :], partX[n][:, 1, :, :], ALU.subtract)\
                        .then_inc(signal[n + "X_low"], 1)
                return emit

            def ffn(i, k, lag):
                w = use(i, "ffn", 0)
                dve.wait_ge(w.filled, w.n + 1)
                if some(i, lag + 1):
                    dve.wait_ge(signal["f_clip"], count(i, lag + 1, "f_clip"))
                dve.tensor_tensor(biased[:, :, :], w[:, :].rearrange("p (t d) -> p t d", t=TT),
                                  fbias[:, :].unsqueeze(1).to_broadcast([P, TT, D]), ALU.add).then_inc(w.drained, 1)

            def f_clip(i, k, lag):
                source = use(i, "ffn", 0)
                dve.wait_ge(source.drained, source.n + 1)
                if some(i, lag + 1):
                    dve.wait_ge(signal["f_sum"], count(i, lag + 1, "f_sum"))
                dve.tensor_scalar(clipped[:, :, :], biased[:, :, :], -CLIP, CLIP, ALU.max, ALU.min).then_inc(signal["f_clip"], 1)

            def f_sum(i, k, lag):
                dve.wait_ge(signal["f_clip"], count(i, lag, "f_clip"))
                if some(i, lag + 1):
                    dve.wait_ge(signal["x3"], count(i, lag + 1, "x3"))
                dve.tensor_tensor(sum3[:, :, :], clipped[:, :, :], x2[:, :, :], ALU.add).then_inc(signal["f_sum"], 1)

            run(dve, {
                "qRest": qRest, "qLow": qLow, "kLow": kLow, "maxS": maxS_, "maxX": maxX_,
                "mS": neg_low("S", negS), "mX": neg_low("X", negX), "t1S": normalise("S"), "t1X": normalise("X"),
                "t3S": residual("S", 1, sum1, x_res, "x_res"), "t3X": residual("X", 2, sum2, x1_res, "x1_kept"),
                "ln1": ln1, "ln2": ln2, "ln3": ln3, "kSum": sum_squares("k"), "qSum": sum_squares("q"),
                "kN": rms("k", kvraw[:, :, 0:D], "kX"), "qN": rms("q", qraw[:, :, :], "qX"),
                "kXRest": kXRest, "qXRest": qXRest, "kXLow": low("k"), "qXLow": low("q"), "ffn": ffn,
                "fClip": f_clip, "fSum": f_sum, "stats1": stats1, "aggr1": aggr1, "stats2": stats2, "aggr2": aggr2,
                "stats3": stats3, "aggr3": aggr3,
            }, set_up)

        @block.gpsimd
        def _(pool):
            def gate():
                pool.sem_inc(passed_pool, 1)

            pool.memset(ident[:, :], 0.0).then_inc(const_set, 1)
            pool.wait_ge(const_set, 1)
            pool.affine_select(out=ident[:, :], in_=ident[:, :], compare_op=ALU.not_equal, fill=1.0, base=0,
                               pattern=[[-1, P]], channel_multiplier=1).then_inc(const_set, 1)
            pool.wait_ge(const_set, 2)
            pool.tensor_copy(identb[:, :], ident[:, :]).then_inc(const_set, 1)
            pool.memset(causal[:, :, :], 0.0).then_inc(const_set, 1)
            pool.wait_ge(const_set, 4)
            pool.affine_select(out=causal[:, :, :], in_=causal[:, :, :], compare_op=ALU.is_ge, fill=MASKED, base=0,
                               pattern=[[0, 4], [-1, P]], channel_multiplier=1).then_inc(const_set, 1)
            pool.memset(kdrop[:, :], -1.0).then_inc(const_set, 1)
            pool.wait_ge(const_set, 6)
            for j, first in enumerate((K_PART1, K_PART2)):
                pool.affine_select(out=kdrop[:, j:j + 1], in_=kdrop[:, j:j + 1], compare_op=ALU.is_ge, fill=0.0,
                                   base=-first, pattern=[[0, 1]], channel_multiplier=1).then_inc(const_set, 1)
            pool.wait_ge(ones_set, 1)

            def mask(i, c, lag):
                if c % 2 == 0:
                    return
                n = c // 2
                pool.wait_ge(signal["expS"], count(i, lag, "expS", c + 1))
                gate()
                if n % 3 < 2:
                    g = 2 * (n // 3) + n % 3
                    pt, heads = ptS0[:, 4 * g:4 * g + 4, 0:P], 4
                else:
                    pt, heads = ptS1[:, 8 * (n // 3):8 * (n // 3) + 8, :], 8
                pool.affine_select(out=pt, in_=pt, compare_op=ALU.is_ge, fill=0.0, base=0,
                                   pattern=[[0, heads], [1, P]], channel_multiplier=-1).then_inc(signal["maskedS"], 1)

            def inverse_root(i, lag, n):
                pool.wait_ge(signal[n + "_ss"], count(i, lag, n + "_ss"))
                if some(i, lag + 1):
                    pool.wait_ge(signal[n + "_rs"], count(i, lag + 1, n + "_rs"))
                gate()
                pool.tensor_scalar(ms[n][:, :], ss[n][:, :], 1.0 / HD, RMS_EPS, ALU.mult, ALU.add)\
                    .then_inc(signal[n + "_ms"], 1)
                if some(i, lag + 1):
                    pool.wait_ge(signal[n + "_norm"], count(i, lag + 1, n + "_norm"))
                pool.wait_ge(signal[n + "_ms"], count(i, lag, n + "_ms"))
                pool.tensor_tensor(rs[n][:, :], ms[n][:, :], halfpow[:, :], ALU.pow).then_inc(signal[n + "_rs"], 1)

            def kn(i, k, lag):
                inverse_root(i, lag, "k")

            def place_v(i, k, lag):
                if some(i, lag + 1):
                    pool.wait_ge(signal["pvX"], count(i, lag + 1, "pvX"))
                source = use(i, "kv", 1)
                pool.wait_ge(source.drained, source.n + 1)
                for t in range(TT):
                    gate()
                    pool.tensor_copy(vaX[:, t, :, 0:HD], kvraw[:, t, D:2 * D].rearrange("p (h d) -> p h d", d=HD))\
                        .then_inc(signal["v_placed"], 1)

            def rstd_of(n):
                def emit(i, lag):
                    pool.wait_ge(signal[f"ln{n}_aggr"], count(i, lag, f"ln{n}_aggr"))
                    if some(i, lag + 1):
                        pool.wait_ge(signal[f"ln{n}_rstd"], count(i, lag + 1, f"ln{n}_rstd"))
                    gate()
                    pool.tensor_scalar(ve[n][:, :], mv[n][:, :, 1], LN_EPS, None, ALU.add)\
                        .then_inc(signal[f"ln{n}_var"], 1)
                    if some(i, lag + 1):
                        pool.wait_ge(signal["x%d" % n], count(i, lag + 1, "x%d" % n))
                    pool.wait_ge(signal[f"ln{n}_var"], count(i, lag, f"ln{n}_var"))
                    pool.tensor_tensor(rstd[n][:, :], ve[n][:, :], halfpow[:, 0:TT], ALU.pow)\
                        .then_inc(signal[f"ln{n}_rstd"], 1)
                return emit

            def keep_x1(i, lag):
                pool.wait_ge(signal["x1"], count(i, lag, "x1"))
                source = use(i, "t3X", 0)
                if source:
                    pool.wait_ge(source.drained, source.n + 1)
                gate()
                pool.tensor_copy(x1_res[:, :, :], x1[:, :, :]).then_inc(signal["x1_kept"], 1)

            run(pool, {
                "qkS": mask, "aggr1": lambda i, k, lag: rstd_of(1)(i, lag), "kSum": kn,
                "qSum": lambda i, k, lag: inverse_root(i, lag, "q"),
                "vX": place_v,
                "aggr2": lambda i, k, lag: rstd_of(2)(i, lag),
                "aggr3": lambda i, k, lag: rstd_of(3)(i, lag),
                "keep": lambda i, k, lag: keep_x1(i, lag),
            })


_IN = ["x", "ctx_1024", "L0_attn_w_attn", "L0_attn_w_proj", "L0_xattn_Wq", "L0_xattn_Wkv", "L0_xattn_Wproj",
       "L0_xattn_q_gamma", "L0_xattn_k_gamma", "L0_ffn_weights", "L0_ffn_scale", "L0_ffn_bias"]


def build(nc):
    shapes = {"x": [B * T, D], "ctx_1024": [B * T, D], "L0_attn_w_attn": [D, D + 2 * HD], "L0_attn_w_proj": [D, D],
              "L0_xattn_Wq": [D, D], "L0_xattn_Wkv": [D, 2 * D], "L0_xattn_Wproj": [D, D], "L0_xattn_q_gamma": [HD],
              "L0_xattn_k_gamma": [HD], "L0_ffn_weights": [D, D], "L0_ffn_scale": [D], "L0_ffn_bias": [D]}
    ins = [nc.dram_tensor("in_" + n, shapes[n], F32, kind="ExternalInput").ap() for n in _IN]
    out = nc.dram_tensor("out", [B * T, D], F32, kind="ExternalOutput").ap()
    spill = {tag: nc.dram_tensor("spill_" + tag, [PARTS, DC, P, T], BF16, kind="Internal").ap()
             for tag in ("qS", "kX", "qX")}
    decoder_program(nc, *ins, out, spill)


def kernel(**inputs):
    import numpy as np
    import concourse.bacc as bacc
    from concourse.bass_utils import run_bass_kernel_spmd

    nc = bacc.Bacc("TRN2", target_bir_lowering=False, num_devices=1)
    build(nc)
    arrays = {}
    for n in _IN:
        a = np.ascontiguousarray(inputs[n])
        arrays["in_" + n] = a.reshape(-1, a.shape[-1]) if a.ndim == 3 else a
    r = run_bass_kernel_spmd(nc, [arrays], core_ids=[0])
    return r.results[0]["out"].reshape(B, T, D)
```
